# Optimizing a Trainium2 kernel written in Bass

```python
import numpy as np
import jax
import jax.numpy as jnp

def _softmax(x, axis=-1):
    return jax.nn.softmax(x, axis=axis)

def _gelu(x):
    return jax.nn.gelu(x, approximate=True)

def _silu(x):
    return jax.nn.silu(x)

def _sigmoid(x):
    return jax.nn.sigmoid(x)

def _layernorm(x, axis=-1, eps=1e-05):
    m = jnp.mean(x, axis=axis, keepdims=True)
    v = jnp.var(x, axis=axis, keepdims=True)
    return (x - m) / jnp.sqrt(v + eps)

def _scatter_add(tgt, idx, src, axis=0):
    return tgt.at[idx].add(src)

def _segment_sum(src, seg, n):
    return jax.ops.segment_sum(src, seg, n)
kernel_name = 'mk_seq_preln_d1_jaxref_r8_11ae5f'

def setup_inputs(seed: int=0):
    np.random.seed(seed)
    _w = jnp.asarray

    def _L0_attn_setup():
        import jax, jax.numpy as jnp
        import numpy as np
        import math
        B, N, D, K = (4, 512, 128, 8)
        key = jax.random.key(seed)
        ks = jax.random.split(key, 9)
        s = 0.02
        return {'summaries': jax.random.normal(ks[0], (B, N, D), dtype=jnp.float32), 'Wq': jax.random.normal(ks[1], (D, D), dtype=jnp.float32) * s, 'bq': jnp.zeros((D,), dtype=jnp.float32), 'Wk': jax.random.normal(ks[2], (D, D), dtype=jnp.float32) * s, 'bk': jnp.zeros((D,), dtype=jnp.float32), 'Wv': jax.random.normal(ks[3], (D, D), dtype=jnp.float32) * s, 'bv': jnp.zeros((D,), dtype=jnp.float32), 'Wo': jax.random.normal(ks[4], (D, D), dtype=jnp.float32) * s, 'bo': jnp.zeros((D,), dtype=jnp.float32)}
    _L0_attn_in = _L0_attn_setup()

    def _L0_ffn_setup():
        import jax, jax.numpy as jnp
        import numpy as np
        DIM = 128
        HEADS = 16
        HD = DIM // HEADS
        M = 32
        E = 4
        K = 2
        HID = 256
        MID = 256
        LB = 0.01
        EPS = 1.1920929e-07

        def _rms(x, w):
            return x * jax.lax.rsqrt(jnp.mean(x * x, axis=-1, keepdims=True) + EPS) * w

        def _gelu(x):
            return jax.nn.gelu(x, approximate=False)
        key = jax.random.key(seed)
        ks = jax.random.split(key, 20)
        d = DIM
        w = lambda k, s: jax.random.normal(k, s, jnp.float32) * 0.02
        return {'x': jax.random.normal(ks[0], (4, 128, d), jnp.float32), 'n1_w': jnp.ones((d,), jnp.float32), 'n2_w': jnp.ones((d,), jnp.float32), 'wq': w(ks[1], (d, d)), 'wk': w(ks[2], (d, d)), 'wv': w(ks[3], (d, d)), 'wo': w(ks[4], (d, d)), 'qn_w': jnp.ones((HD,), jnp.float32), 'kn_w': jnp.ones((HD,), jnp.float32), 'gate_w': w(ks[5], (E, d)), 'e0_up': w(ks[6], (HID, d)), 'e0_down': w(ks[7], (d, HID)), 'e1_w1': w(ks[8], (HID, d)), 'e1_w2': w(ks[9], (HID, d)), 'e1_down': w(ks[10], (d, HID)), 'e2_l1': w(ks[11], (MID, d)), 'e2_l2': w(ks[12], (HID, MID)), 'e2_l3': w(ks[13], (MID, HID)), 'e2_l4': w(ks[14], (d, MID)), 'e3_down': w(ks[15], (d, d)), 'e3_up': w(ks[16], (HID, d)), 'e3_out': w(ks[17], (d, HID))}
    _L0_ffn_in = _L0_ffn_setup()
    _d = {'L0_attn_summaries': _L0_attn_in['summaries'], 'L0_attn_Wq': _L0_attn_in['Wq'], 'L0_attn_bq': _L0_attn_in['bq'], 'L0_attn_Wk': _L0_attn_in['Wk'], 'L0_attn_bk': _L0_attn_in['bk'], 'L0_attn_Wv': _L0_attn_in['Wv'], 'L0_attn_bv': _L0_attn_in['bv'], 'L0_attn_Wo': _L0_attn_in['Wo'], 'L0_attn_bo': _L0_attn_in['bo'], 'L0_ffn_n1_w': _L0_ffn_in['n1_w'], 'L0_ffn_n2_w': _L0_ffn_in['n2_w'], 'L0_ffn_wq': _L0_ffn_in['wq'], 'L0_ffn_wk': _L0_ffn_in['wk'], 'L0_ffn_wv': _L0_ffn_in['wv'], 'L0_ffn_wo': _L0_ffn_in['wo'], 'L0_ffn_qn_w': _L0_ffn_in['qn_w'], 'L0_ffn_kn_w': _L0_ffn_in['kn_w'], 'L0_ffn_gate_w': _L0_ffn_in['gate_w'], 'L0_ffn_e0_up': _L0_ffn_in['e0_up'], 'L0_ffn_e0_down': _L0_ffn_in['e0_down'], 'L0_ffn_e1_w1': _L0_ffn_in['e1_w1'], 'L0_ffn_e1_w2': _L0_ffn_in['e1_w2'], 'L0_ffn_e1_down': _L0_ffn_in['e1_down'], 'L0_ffn_e2_l1': _L0_ffn_in['e2_l1'], 'L0_ffn_e2_l2': _L0_ffn_in['e2_l2'], 'L0_ffn_e2_l3': _L0_ffn_in['e2_l3'], 'L0_ffn_e2_l4': _L0_ffn_in['e2_l4'], 'L0_ffn_e3_down': _L0_ffn_in['e3_down'], 'L0_ffn_e3_up': _L0_ffn_in['e3_up'], 'L0_ffn_e3_out': _L0_ffn_in['e3_out']}
    _x0 = _d['L0_attn_summaries']
    _d['L0_attn_summaries'] = jax.random.normal(jax.random.fold_in(jax.random.key(seed), 1), (2, 1024, 128), dtype=_x0.dtype)
    del _x0
    return _d

def reference(L0_attn_summaries, L0_attn_Wq, L0_attn_bq, L0_attn_Wk, L0_attn_bk, L0_attn_Wv, L0_attn_bv, L0_attn_Wo, L0_attn_bo, L0_ffn_n1_w, L0_ffn_n2_w, L0_ffn_wq, L0_ffn_wk, L0_ffn_wv, L0_ffn_wo, L0_ffn_qn_w, L0_ffn_kn_w, L0_ffn_gate_w, L0_ffn_e0_up, L0_ffn_e0_down, L0_ffn_e1_w1, L0_ffn_e1_w2, L0_ffn_e1_down, L0_ffn_e2_l1, L0_ffn_e2_l2, L0_ffn_e2_l3, L0_ffn_e2_l4, L0_ffn_e3_down, L0_ffn_e3_up, L0_ffn_e3_out):

    def _L0_attn_ref(summaries, Wq, bq, Wk, bk, Wv, bv, Wo, bo):
        import jax, jax.numpy as jnp
        import numpy as np
        import math
        B, N, D, K = (4, 512, 128, 8)
        b_, n_, d_ = summaries.shape
        q = summaries @ Wq + bq
        k = summaries @ Wk + bk
        v = summaries @ Wv + bv
        scores = jnp.einsum('bnd,bmd->bnm', q, k) / math.sqrt(d_)
        causal = jnp.triu(jnp.full((n_, n_), -jnp.inf, dtype=scores.dtype), k=1)
        scores = scores + causal
        topk_vals, topk_idx = jax.lax.top_k(scores, K)
        bi = jnp.arange(b_)[:, None, None]
        ri = jnp.arange(n_)[None, :, None]
        sparse = jnp.full_like(scores, -jnp.inf).at[bi, ri, topk_idx].set(topk_vals)
        attn = jax.nn.softmax(sparse, axis=-1)
        out = jnp.einsum('bnm,bmd->bnd', attn, v)
        return out @ Wo + bo

    def _L0_ffn_ref(x, n1_w, n2_w, wq, wk, wv, wo, qn_w, kn_w, gate_w, e0_up, e0_down, e1_w1, e1_w2, e1_down, e2_l1, e2_l2, e2_l3, e2_l4, e3_down, e3_up, e3_out):
        import jax, jax.numpy as jnp
        import numpy as np
        DIM = 128
        HEADS = 16
        HD = DIM // HEADS
        M = 32
        E = 4
        K = 2
        HID = 256
        MID = 256
        LB = 0.01
        EPS = 1.1920929e-07

        def _rms(x, w):
            return x * jax.lax.rsqrt(jnp.mean(x * x, axis=-1, keepdims=True) + EPS) * w

        def _gelu(x):
            return jax.nn.gelu(x, approximate=False)
        B, T, C = x.shape
        h = _rms(x, n1_w)
        heads = lambda w_: (h @ w_.T).reshape(B, T, HEADS, HD).transpose(0, 2, 1, 3)
        q = _rms(heads(wq), qn_w)
        k = _rms(heads(wk), kn_w)
        v = heads(wv)
        scores = jnp.einsum('bhqd,bhkd->bhqk', q, k) * HD ** (-0.5)
        causal = jnp.tril(jnp.ones((T, T), bool))
        scores = jnp.where(causal[None, None], scores, -jnp.inf)
        attn = jax.nn.softmax(scores, axis=-1)
        ao = jnp.einsum('bhqk,bhkd->bhqd', attn, v).transpose(0, 2, 1, 3).reshape(B, T, C) @ wo.T
        ao = ao.at[:, :, :M].set(0.0)
        x = x + ao
        xf = _rms(x, n2_w).reshape(-1, C)
        N = xf.shape[0]
        logits = jnp.nan_to_num(xf @ gate_w.T)
        probs = jax.nn.softmax(logits, axis=-1)
        topv, topi = jax.lax.top_k(probs, K)
        topv = topv / (topv.sum(-1, keepdims=True) + 1e-08)
        wts = jnp.zeros((N, E), x.dtype).at[jnp.arange(N)[:, None], topi].add(topv)
        o0 = _gelu(xf @ e0_up.T) @ e0_down.T
        o1 = jax.nn.silu(xf @ e1_w1.T) * (xf @ e1_w2.T) @ e1_down.T
        o2 = _gelu(_gelu(_gelu(xf @ e2_l1.T) @ e2_l2.T) @ e2_l3.T) @ e2_l4.T
        o3 = _gelu(_gelu(xf @ e3_down.T) @ e3_up.T) @ e3_out.T
        moe = wts[:, 0:1] * o0 + wts[:, 1:2] * o1 + wts[:, 2:3] * o2 + wts[:, 3:4] * o3
        moe = moe.reshape(B, T, C).at[:, :, :M].set(0.0)
        return x + moe
    x = L0_attn_summaries
    x = x + _L0_attn_ref(_layernorm(x, axis=-1), L0_attn_Wq, L0_attn_bq, L0_attn_Wk, L0_attn_bk, L0_attn_Wv, L0_attn_bv, L0_attn_Wo, L0_attn_bo)
    x = x + _L0_ffn_ref(_layernorm(x, axis=-1), L0_ffn_n1_w, L0_ffn_n2_w, L0_ffn_wq, L0_ffn_wk, L0_ffn_wv, L0_ffn_wo, L0_ffn_qn_w, L0_ffn_kn_w, L0_ffn_gate_w, L0_ffn_e0_up, L0_ffn_e0_down, L0_ffn_e1_w1, L0_ffn_e1_w2, L0_ffn_e1_down, L0_ffn_e2_l1, L0_ffn_e2_l2, L0_ffn_e2_l3, L0_ffn_e2_l4, L0_ffn_e3_down, L0_ffn_e3_up, L0_ffn_e3_out)
    return x

_drawn_inputs = setup_inputs


def setup_inputs(seed=0):
    import zlib

    import numpy as np

    out = dict(_drawn_inputs(seed))
    spreads = {'L0_attn_bq': (0.0, 0.517),
     'L0_attn_bk': (0.0, 0.8),
     'L0_attn_bv': (0.0, 0.379),
     'L0_attn_bo': (0.0, 0.1),
     'L0_ffn_n1_w': (1.0, 0.6),
     'L0_ffn_n2_w': (1.0, 0.6),
     'L0_ffn_qn_w': (1.0, 0.6),
     'L0_ffn_kn_w': (1.0, 0.6)}
    factors = {'L0_attn_Wq': 2.881,
     'L0_attn_Wk': 2.762,
     'L0_attn_Wv': 2.746,
     'L0_ffn_wq': 8.0,
     'L0_ffn_wk': 8.0,
     'L0_ffn_wv': 8.0,
     'L0_ffn_wo': 8.0,
     'L0_ffn_gate_w': 8.0,
     'L0_ffn_e0_up': 8.0,
     'L0_ffn_e0_down': 8.0,
     'L0_ffn_e1_w1': 8.0,
     'L0_ffn_e1_w2': 8.0,
     'L0_ffn_e1_down': 8.0,
     'L0_ffn_e2_l1': 8.0,
     'L0_ffn_e2_l2': 8.0,
     'L0_ffn_e2_l3': 8.0,
     'L0_ffn_e2_l4': 8.0,
     'L0_ffn_e3_down': 8.0,
     'L0_ffn_e3_up': 8.0,
     'L0_ffn_e3_out': 8.0}
    for name, (base, spread) in spreads.items():
        noise = np.random.default_rng([zlib.crc32(name.encode()), seed]).standard_normal(out[name].shape)
        drawn = base * np.exp(spread * noise) if base else spread * noise
        out[name] = jnp.asarray(drawn.astype(out[name].dtype))
    for name, factor in factors.items():
        out[name] = (out[name] * factor).astype(out[name].dtype)
    return out
```

```python
from contextlib import ExitStack

import concourse.bass as bass
from concourse import mybir

F32 = mybir.dt.float32
BF16 = mybir.dt.bfloat16
U32 = mybir.dt.uint32
ALU = mybir.AluOpType
ACT = mybir.ActivationFunctionType
AX_X = mybir.AxisListType.X

P = 128
B, T, D = 2, 1024, 128
NT = B * T // P
TB = T // P
TOPK = 8
H, HD = 16, 8
HG = 4
NG = B * H // HG
CH = 512
HID = 256
E = 4
ZM = 32
ZW = D - ZM
NEG = -1.0e30
MARK = -3.0e38
FMAX = 3.4028234663852886e38
LN_EPS = 1e-5
RMS_EPS = 1.1920929e-07
ROWS = 48
PADR = 96
MROW = 96
EROWS = MROW + 3
Q_PARTS = (0, 0, 0, 1, 1, 2)
K_PARTS = (0, 1, 2, 0, 1, 0)
LAG = 2
STEPS = 12
EUNITS = 2 * STEPS
DIAGS = 16

W_COLS = {}
_at = 0
for _name, _n in (("Wq", D), ("Wk", D), ("Wv", D), ("Wo", D), ("qkv", 3 * D), ("wo", D), ("gate", E),
                  ("e0_up", HID), ("e1_w1", HID), ("e1_w2", HID), ("e2_l1", HID), ("e3_down", D), ("e3_up", HID)):
    W_COLS[_name] = (_at, _n)
    _at += _n
W_ALL = _at
W_ATT = 4 * D
V_COLS = {}
_at = 0
for _name, _n in (("e0_down", D), ("e1_down", D), ("e2_l2", HID), ("e2_l3", HID), ("e2_l4", D), ("e3_out", D)):
    V_COLS[_name] = (_at, _n)
    _at += _n
V_ALL = _at


def key_block_steps():
    out = []
    for c in range(2):
        for kb in range(4 * c + 4):
            diag = kb >= 4 * c
            out.append((c, kb, (kb - 4 * c) * P if diag else 0, diag))
    return out


def max_units():
    out = []
    for qi in range(TB):
        if qi >= 4:
            out += [(qi, j, 1, 0, CH, False) for j in range(HG)]
        w = P * (qi % 4 + 1)
        n = max(1, min(HG, CH // w)) if w != 3 * P else 1
        out += [(qi, j, n, CH * (qi // 4), w, True) for j in range(0, HG, n)]
    return out


KSTEPS = key_block_steps()
MUNITS = max_units()
MUN = len(MUNITS)
MUN_A = sum(u[0] < 4 for u in MUNITS)


def units_of_step(s):
    return range(MUN * s // STEPS, MUN * (s + 1) // STEPS)


STEP_A = next(s for s in range(STEPS) if MUN * (s + 1) // STEPS >= MUN_A)
MROWS_STEP = STEP_A + 2
BACK0_STEP = 8
BACK1_STEP = 3


def build(nc, x, wts, wts2, cols, rows, out):
    ctx = ExitStack()
    with ctx:
        def sb(name, shape, dt=F32):
            return ctx.enter_context(nc.sbuf_tensor(name, shape, dt))

        def sem(name):
            return ctx.enter_context(nc.semaphore(name))

        ps = ctx.enter_context(nc.psum_tensor("ps", [P, 8, CH], F32))
        ident = sb("ident", [P, P])
        identb = sb("identb", [P, P], BF16)
        maskb = sb("maskb", [P, P], BF16)
        w = sb("w", [P, W_ALL])
        w2 = sb("w2", [P, 2, V_ALL])
        col = sb("col", [P, 4])
        row = sb("row", [P, 2 * D + 2 * HD])
        xs = sb("xs", [P, NT, D])
        ys = sb("ys", [P, NT, D])
        tmp = sb("tmp", [P, NT, D])
        tT = sb("tT", [P, NT * P])
        st = sb("st", [P, NT, 6])
        mv = sb("mv", [P, NT, 2])
        sm = sb("sm", [P, 8, NT])
        AR = 14336
        ar = sb("ar", [P, AR])
        qT = ar[:, 0:2048]
        kT = ar[:, 2048:4096]
        vv = ar[:, 4096:6144].rearrange("p (t d) -> p t d", t=NT)
        prob = ar[:, 6144:8192].rearrange("p (n k) -> p n k", n=2)
        repl = ar[:, 8192:10240].rearrange("p (n k) -> p n k", n=2)
        psel = ar[:, 10240:12288].rearrange("p (n k) -> p n k", n=2)
        pselT = ar[:, 12288:14336].rearrange("p (n k) -> p n k", n=2)
        qst = [ar[:, 4096 * u:4096 * u + 2048].bitcast(BF16).rearrange("p (c j t) -> p c j t", c=2, j=HG) for u in range(2)]
        kst = [ar[:, 4096 * u + 2048:4096 * u + 4096].bitcast(BF16).rearrange("p (j t) -> p j t", j=HG) for u in range(2)]
        pt = ar[:, 8192:14336].rearrange("p (n j t) -> p n j t", n=3, j=HG)
        hid = ar[:, 0:28 * CH].rearrange("p (n t) -> p n t", n=28)
        qk = sb("qk", [P, 4, 2 * D])
        sq = sb("sq", [P, 4, 2 * D])
        hs = sb("hs", [P, 4, 4 * 2 * H])
        parts = sb("parts", [P, 3, 4, 2 * D], BF16)
        partT = sb("partT", [P, 3, 2, CH], BF16)
        va = sb("va", [P, NG, TB, HG * HD])
        vg = [sb(f"vg{u}", [P, TB, HG, 32]) for u in range(2)]
        ao = sb("ao", [P, TB, B * D])
        avs = sb("avs", [P, 2, CH])
        rec = sb("rec", [P, 2, 4, HG])
        mxa = sb("mxa", [P, 3, HG, 4])
        mxm = sb("mxm", [P, 2, HG * 4])
        mxp = sb("mxp", [P, 2, 8, HG * 4], BF16)
        mxT = sb("mxT", [P, 2, P], BF16)
        m8 = sb("m8", [P, NT, 8])
        negm = sb("negm", [P, NT])
        den = sb("den", [P, NT])
        rden = sb("rden", [P, NT])
        aT = sb("aT", [P, 2, P])
        gl = sb("gl", [P, 10, NT, E])
        ga = sb("ga", [P, 4, NT])

        split = nc.dram_tensor("split", [6, B * D, T], BF16, kind="Internal").ap()

        def W(name, a=0, b=None):
            o, n = W_COLS[name]
            return w[:, o + a:o + (n if b is None else b)]

        def V(name, r, a=0, b=None):
            o, n = V_COLS[name]
            return w2[:, r, o + a:o + (n if b is None else b)]

        x_in = [sem(f"x_in{b}") for b in range(B)]
        wa_in = sem("wa_in")
        wf_in = sem("wf_in")
        vec_in = sem("vec_in")
        const_ready = sem("const_ready")
        var_ready = sem("var_ready")
        sd_ready = sem("sd_ready")
        xn_ready = sem("xn_ready")
        tr_done = sem("tr_done")
        tT_ready = sem("tT_ready")
        q_done = sem("q_done")
        k_done = sem("k_done")
        v_done = sem("v_done")
        q_ready = sem("q_ready")
        k_ready = sem("k_ready")
        v_ready = sem("v_ready")
        scored = sem("scored")
        chosen = sem("chosen")
        exped = sem("exped")
        psel_ready = sem("psel_ready")
        pT_done = sem("pT_done")
        pT_ready = sem("pT_ready")
        av_a = sem("av_a")
        aT_ready = sem("aT_ready")
        wo_done = sem("wo_done")
        x1_ready = sem("x1_ready")
        vstep = sem("vstep")
        hT_done = sem("hT_done")
        hT_ready = sem("hT_ready")
        qkv_done = sem("qkv_done")
        qkv_read = sem("qkv_read")
        sq_ready = sem("sq_ready")
        ms_ready = sem("ms_ready")
        msd_ready = sem("msd_ready")
        qk_scaled = sem("qk_scaled")
        qk_normed = sem("qk_normed")
        hi_ready = sem("hi_ready")
        r1_ready = sem("r1_ready")
        mid_ready = sem("mid_ready")
        lo_ready = sem("lo_ready")
        spT_done = sem("spT_done")
        spT_ready = sem("spT_ready")
        spT_stored = [sem(f"spT_stored{p}") for p in range(3)]
        pads_ready = sem("pads_ready")
        stack_in = [sem(f"stack_in{u}") for u in range(2)]
        m_scored = sem("m_scored")
        m_reduced = sem("m_reduced")
        max_step = sem("max_step")
        m_parts = sem("m_parts")
        m_rows_done = sem("m_rows_done")
        m_rows_ready = sem("m_rows_ready")
        rows_in = [sem(f"rows_in{h}") for h in range(2)]
        turned = sem("turned")
        e_scored = sem("e_scored")
        e_exped = sem("e_exped")
        unit_taken = sem("unit_taken")
        diag_done = sem("diag_done")
        vg_ready = sem("vg_ready")
        av_done = sem("av_done")
        avs_ready = sem("avs_ready")
        back_done = sem("back_done")
        norm_step = sem("norm_step")
        aoT_done = sem("aoT_done")
        aoT_ready = sem("aoT_ready")
        proj_done = sem("proj_done")
        x2_ready = sem("x2_ready")
        xf_ready = sem("xf_ready")
        xfT_done = sem("xfT_done")
        xfT_ready = sem("xfT_ready")
        gate_done = sem("gate_done")
        gate_exp = sem("gate_exp")
        gmax_ready = sem("gmax_ready")
        hb_done = sem("hb_done")
        hb_read = sem("hb_read")
        glu_ready = sem("glu_ready")
        down_done = sem("down_done")
        out_ready = sem("out_ready")
        out_sent = sem("out_sent")

        block = ctx.enter_context(nc.Block())

        MOE = []
        for hb in range(2):
            MOE.append(("h0", "e0_up", 1, hb, None))
        for hb in range(2):
            MOE.append(("a1", "e2_l1", 1, hb, None))
        for hb in range(2):
            MOE.append(("z1", "e1_w1", 1, hb, None))
        MOE.append(("d3", "e3_down", 1, 0, None))
        for hb in range(2):
            MOE.append(("a2", "e2_l2", 2, hb, "a1"))
        for hb in range(2):
            MOE.append(("z2", "e1_w2", 1, hb, None))
        for hb in range(2):
            MOE.append(("u3", "e3_up", 1, hb, "d3"))
        for hb in range(2):
            MOE.append(("a3", "e2_l3", 2, hb, "a2"))
        NB = len(MOE)
        SLOT = {}
        for name, _, _, hb, _ in MOE:
            SLOT[(name, hb)] = len(SLOT)
        ORDER = {(m[0], m[3]): i for i, m in enumerate(MOE)}

        @block.sync
        def _(sp):
            xt = x.rearrange("b (t p) d -> p (b t) d", p=P)
            for b in range(B):
                sp.dma_start(xs[:, b * TB:(b + 1) * TB, :], xt[:, b * TB:(b + 1) * TB, :]).then_inc(x_in[b], 16)
            for p in range(3):
                sp.wait_ge(spT_stored[p], 16 * 4)
            sp.wait_ge(pads_ready, 3)

            def load_stacks(g, u):
                src = split[:, bass.ds(g * 32, 32), :]
                for p in range(6):
                    one = src[Q_PARTS[p]].rearrange("(j d) (c t) -> d c j t", d=HD, c=2)
                    for c in range(2):
                        sp.dma_start(qst[u][8 * p:8 * p + 8, c], one[:, c]).then_inc(stack_in[u], 16)
                    one = src[3 + K_PARTS[p]].rearrange("(j d) t -> d j t", d=HD)
                    sp.dma_start(kst[u][8 * p:8 * p + 8], one).then_inc(stack_in[u], 16)

            def load_rows(g, u, h):
                sp.wait_ge(m_rows_ready, 2 * g + h + 1)
                sp.dma_start(qst[u][MROW:MROW + 3, h].rearrange("p j (i t) -> p (j i) t", i=4),
                             mxT[0:48, h, :]).then_inc(rows_in[h], 16)

            def half(g, u, more, last=False):
                load_rows(g, u, 1)
                if not last:
                    load_rows(g + 1, 1 - u, 0)
                if more:
                    sp.wait_ge(e_scored, (g + 1) * EUNITS)
                    load_stacks(g + 2, u)

            load_stacks(0, 0)
            load_stacks(1, 1)
            load_rows(0, 0, 0)
            half(0, 0, True)
            with sp.Fori(0, 2) as i:
                half(2 * i + 1, 1, True)
                half(2 * i + 2, 0, True)
            half(5, 1, True)
            half(6, 0, False)
            half(7, 1, False, last=True)
            ot = out.rearrange("b (t p) d -> p (b t) d", p=P)
            for c in range(4):
                sp.wait_ge(out_ready, 4 * (c + 1))
                sp.dma_start(ot[:, 4 * c:4 * c + 4, :], xs[:, 4 * c:4 * c + 4, :]).then_inc(out_sent, 16)
            sp.wait_ge(out_sent, 64)

        @block.gpsimd
        def _(pool):
            pool.memset(ident[:], 0.0).then_inc(const_ready, 1)
            pool.memset(identb[:], 0.0).then_inc(const_ready, 1)
            pool.memset(maskb[:], 0.0).then_inc(const_ready, 1)
            pool.wait_ge(const_ready, 3)
            for m in (ident, identb):
                pool.affine_select(out=m[:], in_=m[:], compare_op=ALU.not_equal, fill=1.0, base=0,
                                   pattern=[[-1, P]], channel_multiplier=1).then_inc(const_ready, 1)
            pool.affine_select(out=maskb[:], in_=maskb[:], compare_op=ALU.is_ge, fill=NEG, base=0,
                               pattern=[[-1, P]], channel_multiplier=1).then_inc(const_ready, 1)
            for u in range(2):
                pool.memset(vg[u][:], 0.0).then_inc(const_ready, 1)
            pool.memset(mxp[:], 0.0)
            pool.wait_ge(const_ready, 8)
            for u in range(2):
                pool.memset(vg[u][:, :, :, HD:HD + 1], 1.0).then_inc(const_ready, 1)

            pool.wait_ge(vec_in, 32)
            for z in range(4):
                pool.wait_ge(qkv_read, 4 * (z + 1))
                pool.tensor_tensor(sq[:], qk[:], qk[:], ALU.mult).then_inc(sq_ready, 1)
                pool.wait_ge(qk_scaled, z + 1)
                for s in range(2):
                    v = qk[:, :, s * D:(s + 1) * D].rearrange("p t (h d) -> p t h d", h=H)
                    nw = row[:, 2 * D + s * HD:2 * D + (s + 1) * HD].unsqueeze(1).unsqueeze(1).to_broadcast([P, 4, H, HD])
                    pool.tensor_tensor(v, v, nw, ALU.mult).then_inc(qk_normed, 1)
            pool.wait_ge(x1_ready, NT)
            pool.wait_ge(qk_normed, 8)
            pool.memset(ar[:, 0:8192], 0.0).then_inc(pads_ready, 1)
            pool.wait_ge(pads_ready, 1)
            for u in range(2):
                pool.memset(kst[u][MROW:MROW + 3], 1.0).then_inc(pads_ready, 1)
            pool.wait_ge(pads_ready, 3)

            def copy_v(g, u):
                pool.tensor_copy(vg[u][:, :, :, 0:HD],
                                 va[:, bass.ds(g, 1)].rearrange("p o k (j d) -> p (o k) j d", j=HG)).then_inc(vg_ready, 1)

            pool.wait_ge(qkv_read, NT)
            copy_v(0, 0)

            def run(g, u, first=False, last=False):
                for s, (c, kb, off, diag) in enumerate(KSTEPS):
                    if diag:
                        for jj in range(2):
                            pool.wait_ge(e_exped, g * EUNITS + 2 * s + jj + 1)
                            pool.sem_inc(unit_taken, 1)
                            v = pt[:, s % 3, 2 * jj:2 * jj + 2, off:off + P]
                            pool.affine_select(out=v, in_=v, compare_op=ALU.is_ge, fill=0.0, base=0,
                                               pattern=[[0, 2], [1, P]], channel_multiplier=-1).then_inc(diag_done, 1)
                    if s == 4 and not last:
                        if not first:
                            pool.wait_ge(av_done, g * STEPS)
                        copy_v(g + 1, 1 - u)

            run(0, 0, first=True)
            with pool.Fori(0, 3) as i:
                run(2 * i + 1, 1)
                run(2 * i + 2, 0)
            run(7, 1, last=True)

        @block.scalar
        def _(act):
            act.dma_start(w[:, 0:W_ATT], wts[:, 0:W_ATT]).then_inc(wa_in, 16)
            act.dma_start(col[:], cols).then_inc(vec_in, 16)
            act.dma_start(row[:], rows.to_broadcast([P, 2 * D + 2 * HD])).then_inc(vec_in, 16)
            act.dma_start(w[:, W_ATT:W_ALL], wts[:, W_ATT:W_ALL]).then_inc(wf_in, 16)
            act.dma_start(w2[:], wts2.rearrange("(r p) n -> p r n", p=P)).then_inc(wf_in, 16)
            act.wait_ge(vec_in, 32)
            act.wait_ge(var_ready, 1)
            nc.scalar.activation(sm[:, 1, :], sm[:, 0, :], ACT.Sqrt).then_inc(sd_ready, 1)
            for c in range(4):
                act.wait_ge(tr_done, c + 1)
                nc.scalar.copy(tT[:, c * CH:(c + 1) * CH], ps[:, c % 2, :]).then_inc(tT_ready, 1)
            for c in range(4):
                act.wait_ge(q_done, c + 1)
                nc.scalar.activation(qT[:, c * CH:(c + 1) * CH], ps[:, 2 + c % 2, :], ACT.Identity,
                                     bias=col[:, 0:1]).then_inc(q_ready, 1)
            for t in range(NT + 2):
                if t < NT:
                    wdt = P * (t % TB + 1)
                    act.wait_ge(chosen, t + 1)
                    if t >= 2:
                        act.wait_ge(psel_ready, t - 1)
                    nc.scalar.activation(prob[:, t % 2, 0:wdt], ps[:, 2 * (t % 2):2 * (t % 2) + 2, :].rearrange("p a b -> p (a b)")[:, 0:wdt],
                                         ACT.Exp, bias=negm[:, t:t + 1], scale=float(D) ** -0.5).then_inc(exped, 1)
                if 1 <= t < NT + 1:
                    n = t - 1
                    wdt = P * (n % TB + 1)
                    act.wait_ge(pT_done, n + 1)
                    if n >= 2:
                        act.wait_ge(av_a, n - 1)
                    nc.scalar.copy(pselT[:, n % 2, 0:wdt], ps[:, 4:6, :].rearrange("p a b -> p (a b)")[:, 0:wdt]).then_inc(pT_ready, 1)
                if t >= 2:
                    n = t - 2
                    act.wait_ge(av_a, n + 1)
                    if n >= 2:
                        act.wait_ge(wo_done, n - 1)
                    nc.scalar.copy(aT[:, n % 2, :], ps[:, 6, 0:P]).then_inc(aT_ready, 1)

            for k in range(2):
                act.wait_ge(var_ready, 2 + k)
                nc.scalar.activation(sm[:, 1 + 2 * k, :], sm[:, 2 * k, :], ACT.Sqrt).then_inc(sd_ready, 1)
            for c in range(4):
                act.wait_ge(hT_done, c + 1)
                nc.scalar.activation(tT[:, c * CH:(c + 1) * CH], ps[:, c % 2, :], ACT.Copy, scale=col[:, 2:3]).then_inc(hT_ready, 1)
            for z in range(4):
                for t in range(4 * z, 4 * z + 4):
                    act.wait_ge(qkv_done, t + 1)
                    if t == 4 * z and z:
                        act.wait_ge(lo_ready, z)
                    nc.scalar.copy(qk[:, t % 4, :], ps[:, 2 + t % 2, 0:2 * D])
                    nc.scalar.copy(va[:, 4 * (t // TB):4 * (t // TB) + 4, t % TB, :],
                                   ps[:, 2 + t % 2, 2 * D:3 * D].rearrange("p (g d) -> p g d", g=4)).then_inc(qkv_read, 1)
                act.wait_ge(ms_ready, z + 1)
                nc.scalar.activation(hs[:, 1, :], hs[:, 0, :], ACT.Sqrt).then_inc(msd_ready, 1)
                act.wait_ge(qk_normed, 2 * (z + 1))
                if z:
                    act.wait_ge(spT_done, 3 * z)
                nc.scalar.copy(parts[:, 0], qk[:]).then_inc(hi_ready, 1)
                act.wait_ge(r1_ready, z + 1)
                nc.scalar.copy(parts[:, 1], qk[:]).then_inc(mid_ready, 1)
                for p in range(3):
                    act.wait_ge(spT_done, 3 * z + p + 1)
                    if z:
                        act.wait_ge(spT_stored[p], 16 * z)
                    nc.scalar.copy(partT[:, p].rearrange("p s t -> p (s t)"),
                                   ps[:, 4 + (3 * z + p) % 2, :].bitcast(BF16)).then_inc(spT_ready, 1)
                    act.wait_ge(spT_ready, 3 * z + p + 1)
                    b, q = z // 2, z % 2
                    act.dma_start(split.rearrange("(s q) f t -> q f s t", s=2)[p][b * D:(b + 1) * D, :, q * CH:(q + 1) * CH],
                                  partT[:, p]).then_inc(spT_stored[p], 16)

            def row_copy(g, h, first=False):
                act.wait_ge(m_rows_done, 2 * g + h + 1)
                if not first:
                    act.wait_ge(rows_in[h], 16 * g)
                nc.scalar.copy(mxT[0:48, h, :], ps[0:48, 7, 0:64].bitcast(BF16)).then_inc(m_rows_ready, 1)

            def run(g, first=False, last=False):
                for s, (c, kb, off, diag) in enumerate(KSTEPS):
                    for jj in range(2):
                        act.wait_ge(e_scored, g * EUNITS + 2 * s + jj + 1)
                        if jj == 0 and not (first and s < 3):
                            act.wait_ge(av_done, g * STEPS + s - 2)
                        nc.scalar.activation(pt[:, s % 3, 2 * jj:2 * jj + 2, off:CH], ps[:, 2 * jj:2 * jj + 2, off:CH],
                                             ACT.Exp, scale=float(HD) ** -0.5).then_inc(e_exped, 1)
                    if s == 1:
                        row_copy(g, 1, first)
                    if s == MROWS_STEP and not last:
                        row_copy(g + 1, 0)

            row_copy(0, 0, first=True)
            run(0, first=True)
            with act.Fori(0, 3) as i:
                run(2 * i + 1)
                run(2 * i + 2)
            run(7, last=True)

            for c in range(4):
                act.wait_ge(aoT_done, c + 1)
                nc.scalar.copy(tT[:, c * CH:(c + 1) * CH], ps[:, c % 2, :]).then_inc(aoT_ready, 1)
            act.wait_ge(var_ready, 4)
            nc.scalar.activation(sm[:, 1, :], sm[:, 0, :], ACT.Sqrt).then_inc(sd_ready, 1)
            for c in range(4):
                act.wait_ge(xfT_done, c + 1)
                nc.scalar.activation(tT[:, c * CH:(c + 1) * CH], ps[:, c % 2, :], ACT.Copy, scale=col[:, 3:4]).then_inc(xfT_ready, 1)
            act.wait_ge(gmax_ready, 1)
            nc.scalar.activation(gl[:, 2], gl[:, 1], ACT.Exp).then_inc(gate_exp, 1)
            for c in range(4):
                for i, (name, wn, nr, hb, src) in enumerate(MOE):
                    n = c * NB + i
                    act.wait_ge(hb_done, n + 1)
                    if c and i == 0:
                        act.wait_ge(down_done, 4 * c)
                    o = hid[:, SLOT[(name, hb)], :]
                    bank = ps[:, n % 6, :]
                    if name == "z1":
                        nc.scalar.activation(o, bank, ACT.Tanh, scale=0.5).then_inc(hb_read, 1)
                    elif name == "z2":
                        nc.scalar.copy(o, bank).then_inc(hb_read, 1)
                    else:
                        nc.scalar.activation(o, bank, ACT.Gelu).then_inc(hb_read, 1)

        @block.vector
        def _(dve):
            v = nc.vector
            count = [0]

            def link(ins):
                count[0] += 1
                ins.then_inc(vstep, 1)
                dve.wait_ge(vstep, count[0])

            def rsqrt(out_, val, root, scratch, ready):
                dve.wait_ge(*ready)
                link(v.reciprocal(out_, root))
                link(v.tensor_tensor(scratch, out_, out_, ALU.mult))
                link(v.tensor_tensor(scratch, scratch, val, ALU.mult))
                link(v.tensor_scalar(scratch, scratch, -0.5, 1.5, ALU.mult, ALU.add))
                link(v.tensor_tensor(out_, out_, scratch, ALU.mult))

            def stats(src, tiles):
                for t in tiles:
                    last = v.bn_stats(st[:, t, :], src[:, t, :])
                link(last)
                for t in tiles:
                    last = v.bn_aggr(mv[:, t, :], st[:, t, :])
                link(last)

            dve.wait_ge(const_ready, 10)
            for b in range(B):
                dve.wait_ge(x_in[b], 16)
                stats(xs, range(b * TB, (b + 1) * TB))
            v.tensor_scalar(sm[:, 0, :], mv[:, :, 1], LN_EPS, None, ALU.add).then_inc(var_ready, 1)
            rsqrt(sm[:, 4, :], sm[:, 0, :], sm[:, 1, :], sm[:, 7, :], (sd_ready, 1))
            for t in range(NT):
                v.tensor_scalar(tmp[:, t, :], xs[:, t, :], mv[:, t, 0:1], sm[:, 4, t:t + 1], ALU.subtract, ALU.mult).then_inc(xn_ready, 1)
            dve.wait_ge(vec_in, 32)
            dve.wait_ge(xn_ready, NT)
            link(v.tensor_tensor(xs[:], xs[:], row[:, D:2 * D].unsqueeze(1).to_broadcast([P, NT, D]), ALU.add))
            for c in range(4):
                dve.wait_ge(k_done, c + 1)
                v.tensor_scalar(kT[:, c * CH:(c + 1) * CH], ps[:, 4 + c % 2, :], col[:, 1:2], None, ALU.add).then_inc(k_ready, 1)
                dve.wait_ge(v_done, c + 1)
                v.tensor_tensor(vv[:, 4 * c:4 * c + 4, :], ps[:, 6 + c % 2, :].rearrange("p (t d) -> p t d", t=4),
                                row[:, 0:D].unsqueeze(1).to_broadcast([P, 4, D]), ALU.add).then_inc(v_ready, 1)
            for t in range(NT + 3):
                if t < NT:
                    wdt = P * (t % TB + 1)
                    dve.wait_ge(scored, t + 1)
                    s = ps[:, 2 * (t % 2):2 * (t % 2) + 2, :].rearrange("p a b -> p (a b)")[:, 0:wdt]
                    link(v.max(m8[:, t, :], s))
                    if t >= 2:
                        dve.wait_ge(psel_ready, t - 1)
                    v.tensor_scalar(negm[:, t:t + 1], m8[:, t, 0:1], -float(D) ** -0.5, None, ALU.mult)
                    v.match_replace(out=repl[:, t % 2, 0:wdt], in_to_replace=m8[:, t, :], in_values=s, imm_value=MARK).then_inc(chosen, 1)
                if 1 <= t < NT + 1:
                    n = t - 1
                    wdt = P * (n % TB + 1)
                    dve.wait_ge(exped, n + 1)
                    dve.wait_ge(chosen, n + 1)
                    if n >= 2:
                        dve.wait_ge(pT_done, n - 1)
                    v.scalar_tensor_tensor(out=psel[:, n % 2, 0:wdt], in0=repl[:, n % 2, 0:wdt], scalar=MARK, in1=prob[:, n % 2, 0:wdt],
                                           op0=ALU.is_equal, op1=ALU.mult, accum_out=den[:, n:n + 1]).then_inc(psel_ready, 1)
                if t >= 3:
                    n = t - 3
                    dve.wait_ge(psel_ready, n + 1)
                    link(v.reciprocal(rden[:, n:n + 1], den[:, n:n + 1]))
                    dve.wait_ge(wo_done, n + 1)
                    v.scalar_tensor_tensor(out=xs[:, n, :], in0=ps[:, 7, 0:D], scalar=rden[:, n:n + 1], in1=xs[:, n, :],
                                           op0=ALU.mult, op1=ALU.add).then_inc(x1_ready, 1)
            dve.wait_ge(x1_ready, NT)

            stats(xs, range(NT))
            link(v.tensor_scalar(sm[:, 0, :], mv[:, :, 1], LN_EPS, None, ALU.add))
            v.tensor_copy(sm[:, 6, :], mv[:, :, 1]).then_inc(var_ready, 1)
            rsqrt(sm[:, 4, :], sm[:, 0, :], sm[:, 1, :], sm[:, 7, :], (sd_ready, 2))
            link(v.tensor_tensor(sm[:, 2, :], sm[:, 4, :], sm[:, 4, :], ALU.mult))
            link(v.tensor_tensor(sm[:, 2, :], sm[:, 2, :], sm[:, 6, :], ALU.mult))
            v.tensor_scalar(sm[:, 2, :], sm[:, 2, :], RMS_EPS, None, ALU.add).then_inc(var_ready, 1)
            rsqrt(sm[:, 5, :], sm[:, 2, :], sm[:, 3, :], sm[:, 7, :], (sd_ready, 3))
            link(v.tensor_tensor(sm[:, 5, :], sm[:, 5, :], sm[:, 4, :], ALU.mult))
            for t in range(NT):
                v.tensor_scalar(tmp[:, t, :], xs[:, t, :], mv[:, t, 0:1], sm[:, 5, t:t + 1], ALU.subtract, ALU.mult).then_inc(xn_ready, 1)
            for t in range(NT):
                last = v.tensor_scalar(ys[:, t, :], xs[:, t, :], mv[:, t, 0:1], sm[:, 4, t:t + 1], ALU.subtract, ALU.mult)
            link(last)
            for z in range(4):
                if z:
                    dve.wait_ge(lo_ready, z)
                dve.wait_ge(sq_ready, z + 1)
                link(v.tensor_reduce(hs[:, 2, :], sq[:].rearrange("p t (h d) -> p (t h) d", d=HD), AX_X, ALU.add))
                v.tensor_scalar(hs[:, 0, :], hs[:, 2, :], 1.0 / HD, RMS_EPS, ALU.mult, ALU.add).then_inc(ms_ready, 1)
                rsqrt(hs[:, 2, :], hs[:, 0, :], hs[:, 1, :], hs[:, 3, :], (msd_ready, z + 1))
                q4 = qk[:].rearrange("p t (h d) -> p (t h) d", d=HD)
                v.tensor_tensor(q4, q4, hs[:, 2, :].unsqueeze(2).to_broadcast([P, 8 * H, HD]), ALU.mult).then_inc(qk_scaled, 1)
                dve.wait_ge(hi_ready, z + 1)
                v.tensor_tensor(qk[:], qk[:], parts[:, 0], ALU.subtract).then_inc(r1_ready, 1)
                dve.wait_ge(mid_ready, z + 1)
                v.tensor_tensor(parts[:, 2], qk[:], parts[:, 1], ALU.subtract).then_inc(lo_ready, 1)

            def reduce_unit(g, n, first=False):
                qi, j, nh, k0, wdt, diag = MUNITS[n]
                if n == 0 and not first:
                    dve.wait_ge(max_step, 8 * g - 3)
                dve.wait_ge(m_scored, g * MUN + n + 1)
                which = 0 if qi < 4 else (2 if diag else 1)
                v.tensor_reduce(mxa[:, which, j:j + nh, qi % 4], ps[:, 4 + n % 2, 0:nh * wdt].rearrange("p (j k) -> p j k", j=nh),
                                AX_X, ALU.max).then_inc(m_reduced, 1)

            def split_maxima(g, h, first=False):
                a = mxa[:, 0 if h == 0 else 1].rearrange("p j i -> p (j i)")
                b = mxa[:, 0 if h == 0 else 2].rearrange("p j i -> p (j i)")
                base = (2 * g + h) * 4
                dve.wait_ge(m_reduced, g * MUN + (MUN_A if h == 0 else MUN))
                if not (first and h == 0):
                    dve.wait_ge(m_parts, 2 * g + h)
                v.tensor_tensor(mxm[:, 0], a, b, ALU.max).then_inc(max_step, 1)
                dve.wait_ge(max_step, base + 1)
                if not first:
                    dve.wait_ge(m_rows_done, 2 * g + h - 1)
                v.tensor_scalar(mxp[:, h, 0], mxm[:, 0], -1.0, None, ALU.mult).then_inc(max_step, 1)
                dve.wait_ge(max_step, base + 2)
                v.scalar_tensor_tensor(out=mxm[:, 1], in0=mxm[:, 0], scalar=-1.0, in1=mxp[:, h, 0],
                                       op0=ALU.mult, op1=ALU.subtract).then_inc(max_step, 1)
                dve.wait_ge(max_step, base + 3)
                v.tensor_copy(mxp[:, h, 1], mxm[:, 1]).then_inc(max_step, 1)
                dve.wait_ge(max_step, base + 4)
                v.tensor_tensor(mxp[:, h, 2], mxm[:, 1], mxp[:, h, 1], ALU.subtract).then_inc(m_parts, 1)

            def take_sums(g, c, first=False):
                dve.wait_ge(av_done, g * STEPS + (4 if c == 0 else STEPS))
                if not first:
                    dve.wait_ge(back_done, 2 * g + c)
                v.tensor_copy(avs[:, c, :], ps[:, 6, :]).then_inc(avs_ready, 1)

            def normalise(g, c, first=False):
                dve.wait_ge(back_done, 2 * g + c + 1)
                t4 = ps[:, 7, :].rearrange("p (i j d) -> p i j d", i=4, j=HG)
                if not first:
                    dve.wait_ge(turned, 2 * g + c)
                v.reciprocal(rec[:, c], t4[:, :, :, HD]).then_inc(norm_step, 1)
                dve.wait_ge(norm_step, 2 * g + c + 1)
                o = ao[:, 4 * c:4 * c + 4, bass.ds(g * HG * HD, HG * HD)].rearrange("p i (j d) -> p i j d", j=HG)
                v.tensor_tensor(o, t4[:, :, :, 0:HD], rec[:, c].unsqueeze(3).to_broadcast([P, 4, HG, HD]), ALU.mult).then_inc(turned, 1)

            def run(g, first=False, last=False):
                for s in range(STEPS):
                    if s == 2 and not first:
                        take_sums(g - 1, 1)
                    if s == BACK1_STEP + 1 and not first:
                        normalise(g - 1, 1)
                    if s == 4 + LAG:
                        take_sums(g, 0, first)
                    if s == BACK0_STEP + 1:
                        normalise(g, 0, first)
                    if not last:
                        for n in units_of_step(s):
                            reduce_unit(g + 1, n)
                        if s == STEP_A:
                            split_maxima(g + 1, 0)
                if not last:
                    split_maxima(g + 1, 1)

            for n in range(MUN):
                reduce_unit(0, n, first=True)
                if n == MUN_A - 1:
                    split_maxima(0, 0, first=True)
            split_maxima(0, 1, first=True)
            run(0, first=True)
            with dve.Fori(0, 3) as i:
                run(2 * i + 1)
                run(2 * i + 2)
            run(7, last=True)
            take_sums(7, 1)
            normalise(7, 1)
            dve.wait_ge(turned, 2 * NG)

            for t in range(NT):
                dve.wait_ge(proj_done, t + 1)
                v.tensor_tensor(ys[:, t, ZM:D], ys[:, t, ZM:D], ps[:, 2 + t % 2, 0:ZW], ALU.add).then_inc(x2_ready, 1)
            dve.wait_ge(x2_ready, NT)
            stats(ys, range(NT))
            link(v.tensor_tensor(sm[:, 2, :], mv[:, :, 0], mv[:, :, 0], ALU.mult))
            link(v.tensor_tensor(sm[:, 2, :], sm[:, 2, :], mv[:, :, 1], ALU.add))
            v.tensor_scalar(sm[:, 0, :], sm[:, 2, :], RMS_EPS, None, ALU.add).then_inc(var_ready, 1)
            rsqrt(sm[:, 4, :], sm[:, 0, :], sm[:, 1, :], sm[:, 7, :], (sd_ready, 4))
            for t in range(NT):
                v.tensor_scalar(tmp[:, t, :], ys[:, t, :], sm[:, 4, t:t + 1], None, ALU.mult).then_inc(xf_ready, 1)
            link(v.tensor_tensor(xs[:], xs[:], ys[:], ALU.add))
            dve.wait_ge(gate_done, 1)
            raw, logit, num, prb, win, cmp_ = (gl[:, i] for i in range(6))
            link(v.tensor_copy(raw, ps[:, 6, 0:NT * E].rearrange("p (t e) -> p t e", t=NT)))
            link(v.tensor_tensor(cmp_, raw, raw, ALU.is_equal))
            link(v.memset(logit, 0.0))
            link(v.copy_predicated(logit, cmp_.bitcast(U32), raw))
            link(v.tensor_scalar(logit, logit, FMAX, -FMAX, ALU.min, ALU.max))
            link(v.tensor_reduce(ga[:, 0], logit, AX_X, ALU.max))
            v.tensor_tensor(logit, logit, ga[:, 0].unsqueeze(2).to_broadcast([P, NT, E]), ALU.subtract).then_inc(gmax_ready, 1)
            dve.wait_ge(gate_exp, 1)
            link(v.tensor_reduce(ga[:, 1], num, AX_X, ALU.add))
            link(v.reciprocal(ga[:, 2], ga[:, 1]))
            link(v.tensor_tensor(prb, num, ga[:, 2].unsqueeze(2).to_broadcast([P, NT, E]), ALU.mult))
            link(v.memset(win, 0.0))
            for a in range(E):
                for b in range(a + 1, E):
                    link(v.tensor_tensor(cmp_[:, :, 0], prb[:, :, a], prb[:, :, b], ALU.is_ge))
                    link(v.tensor_tensor(win[:, :, a], win[:, :, a], cmp_[:, :, 0], ALU.add))
                    link(v.scalar_tensor_tensor(out=win[:, :, b], in0=win[:, :, b], scalar=1.0, in1=cmp_[:, :, 0],
                                                op0=ALU.add, op1=ALU.subtract))
            link(v.scalar_tensor_tensor(out=prb, in0=win, scalar=2.0, in1=prb, op0=ALU.is_ge, op1=ALU.mult))
            link(v.tensor_reduce(ga[:, 1], prb, AX_X, ALU.add))
            link(v.tensor_scalar(ga[:, 1], ga[:, 1], 1e-8, None, ALU.add))
            link(v.reciprocal(ga[:, 2], ga[:, 1]))
            link(v.tensor_tensor(prb, prb, ga[:, 2].unsqueeze(2).to_broadcast([P, NT, E]), ALU.mult))

            for c in range(4):
                for hb in range(2):
                    t1 = hid[:, SLOT[("z1", hb)], :]
                    dve.wait_ge(hb_read, c * NB + ORDER[("z1", hb)] + 1)
                    v.scalar_tensor_tensor(out=t1, in0=t1, scalar=1.0, in1=ps[:, (c * NB + ORDER[("z1", hb)]) % 6, :],
                                           op0=ALU.add, op1=ALU.mult).then_inc(glu_ready, 1)
                for hb in range(2):
                    t1 = hid[:, SLOT[("z1", hb)], :]
                    dve.wait_ge(hb_read, c * NB + ORDER[("z2", hb)] + 1)
                    dve.wait_ge(glu_ready, 4 * c + hb + 1)
                    v.scalar_tensor_tensor(out=t1, in0=hid[:, SLOT[("z2", hb)], :], scalar=0.5, in1=t1,
                                           op0=ALU.mult, op1=ALU.mult).then_inc(glu_ready, 1)
                for t in range(4 * c, 4 * c + 4):
                    dve.wait_ge(down_done, t + 1)
                    for e in range(E):
                        ins = v.scalar_tensor_tensor(out=xs[:, t, ZM:D], in0=ps[:, 6 + t % 2, e * ZW:(e + 1) * ZW], scalar=prb[:, t, e:e + 1],
                                                     in1=xs[:, t, ZM:D], op0=ALU.mult, op1=ALU.add)
                        if e < E - 1:
                            link(ins)
                        else:
                            ins.then_inc(out_ready, 1)

        @block.tensor
        def _(pe):
            mm = nc.tensor.matmul

            def turn(dst, src):
                return nc.tensor.transpose(dst, src, ident[:])

            pe.wait_ge(const_ready, 10)
            for c in range(4):
                if c >= 2:
                    pe.wait_ge(tT_ready, c - 1)
                for i in range(4):
                    t = 4 * c + i
                    pe.wait_ge(xn_ready, t + 1)
                    last = turn(ps[:, c % 2, i * P:(i + 1) * P], tmp[:, t, :])
                last.then_inc(tr_done, 1)
            pe.wait_ge(wa_in, 16)
            for c in range(4):
                pe.wait_ge(tT_ready, c + 1)
                r = tT[:, c * CH:(c + 1) * CH]
                if c >= 2:
                    pe.wait_ge(q_ready, c - 1)
                mm(ps[:, 2 + c % 2, :], W("Wq"), r, start=True, stop=True).then_inc(q_done, 1)
                if c >= 2:
                    pe.wait_ge(k_ready, c - 1)
                mm(ps[:, 4 + c % 2, :], W("Wk"), r, start=True, stop=True).then_inc(k_done, 1)
                if c >= 2:
                    pe.wait_ge(v_ready, c - 1)
                for i in range(4):
                    t = 4 * c + i
                    last = mm(ps[:, 6 + c % 2, i * P:(i + 1) * P], tT[:, t * P:(t + 1) * P], W("Wv"), start=True, stop=True)
                last.then_inc(v_done, 1)
            pe.wait_ge(q_ready, 4)
            pe.wait_ge(k_ready, 4)
            pe.wait_ge(v_ready, 4)
            for t in range(NT + 3):
                if t < NT:
                    b, qi = t // TB, t % TB
                    if t >= 2:
                        pe.wait_ge(exped, t - 1)
                    for k0 in range(0, P * (qi + 1), CH):
                        n = min(CH, P * (qi + 1) - k0)
                        bank = ps[:, 2 * (t % 2) + k0 // CH, :]
                        diag = k0 + n == P * (qi + 1)
                        last = mm(bank[:, 0:n], qT[:, t * P:(t + 1) * P], kT[:, b * T + k0:b * T + k0 + n], start=True, stop=not diag)
                        if diag:
                            last = mm(bank[:, n - P:n], identb[:], maskb[:], start=False, stop=True)
                    last.then_inc(scored, 1)
                if 1 <= t < NT + 1:
                    n = t - 1
                    pe.wait_ge(psel_ready, n + 1)
                    if n >= 1:
                        pe.wait_ge(pT_ready, n)
                    for kb in range(n % TB + 1):
                        last = turn(ps[:, 4 + kb // 4, (kb % 4) * P:(kb % 4 + 1) * P], psel[:, n % 2, kb * P:(kb + 1) * P])
                    last.then_inc(pT_done, 1)
                if 2 <= t < NT + 2:
                    n = t - 2
                    pe.wait_ge(pT_ready, n + 1)
                    if n >= 1:
                        pe.wait_ge(aT_ready, n)
                    nk = n % TB + 1
                    for kb in range(nk):
                        last = mm(ps[:, 6, 0:P], vv[:, (n // TB) * TB + kb, :], pselT[:, n % 2, kb * P:(kb + 1) * P],
                                  start=(kb == 0), stop=(kb == nk - 1))
                    last.then_inc(av_a, 1)
                if t >= 3:
                    n = t - 3
                    pe.wait_ge(aT_ready, n + 1)
                    if n >= 1:
                        pe.wait_ge(x1_ready, n)
                    ins = mm(ps[:, 7, 0:D], aT[:, n % 2, :], W("Wo"), start=True, stop=True)
                    ins.then_inc(wo_done, 1)

            for c in range(4):
                if c >= 2:
                    pe.wait_ge(hT_ready, c - 1)
                for i in range(4):
                    t = 4 * c + i
                    pe.wait_ge(xn_ready, NT + t + 1)
                    last = turn(ps[:, c % 2, i * P:(i + 1) * P], tmp[:, t, :])
                last.then_inc(hT_done, 1)
            pe.wait_ge(wf_in, 32)
            for z in range(4):
                pe.wait_ge(hT_ready, z + 1)
                for t in range(4 * z, 4 * z + 4):
                    if t >= 2:
                        pe.wait_ge(qkv_read, t - 1)
                    mm(ps[:, 2 + t % 2, 0:3 * D], tT[:, t * P:(t + 1) * P], W("qkv"), start=True, stop=True).then_inc(qkv_done, 1)
                pe.wait_ge(lo_ready, z + 1)
                for p in range(3):
                    n = 3 * z + p
                    if n >= 2:
                        pe.wait_ge(spT_ready, n - 1)
                    bank = ps[:, 4 + n % 2, :].bitcast(BF16)
                    for s in range(2):
                        for i in range(4):
                            last = nc.tensor.transpose(bank[:, s * CH + i * P:s * CH + (i + 1) * P], parts[:, p, i, s * D:(s + 1) * D], identb[:])
                    last.then_inc(spT_done, 1)

            def max_unit(g, u, n, first=False):
                qi, j, nh, k0, wdt, diag = MUNITS[n]
                if not (first and n < 2):
                    pe.wait_ge(m_reduced, g * MUN + n - 1)
                bank = ps[:, 4 + n % 2, :]
                for a in range(nh):
                    last = mm(bank[:, a * wdt:(a + 1) * wdt], qst[u][0:PADR, qi // 4, j + a, (qi % 4) * P:(qi % 4 + 1) * P],
                              kst[u][0:PADR, j + a, k0:k0 + wdt], start=True, stop=not diag)
                    if diag:
                        last = mm(bank[:, (a + 1) * wdt - P:(a + 1) * wdt], identb[:], maskb[:], start=False, stop=True)
                last.then_inc(m_scored, 1)

            def row_copy(g, h):
                pe.wait_ge(m_parts, 2 * g + h + 1)
                bank = ps[:, 7, 0:64].bitcast(BF16)
                nc.tensor.transpose(bank, mxp[:, h].rearrange("p a b -> p (a b)"), identb[:]).then_inc(m_rows_done, 1)

            def back(g, c):
                pe.wait_ge(avs_ready, 2 * g + c + 1)
                for i in range(4):
                    last = turn(ps[:, 7, i * P:(i + 1) * P], avs[:, c, i * P:(i + 1) * P])
                last.then_inc(back_done, 1)

            def values(g, u, s, first=False):
                c, kb, off, diag = KSTEPS[s]
                if kb == 0:
                    if not (first and c == 0):
                        pe.wait_ge(avs_ready, 2 * g + c)
                    if c == 0:
                        pe.wait_ge(vg_ready, g + 1)
                if diag:
                    nd = sum(KSTEPS[i][3] for i in range(s + 1))
                    pe.wait_ge(diag_done, g * DIAGS + 2 * nd)
                else:
                    pe.wait_ge(e_exped, g * EUNITS + 2 * s + 2)
                for j in range(HG):
                    last = mm(ps[32 * j:32 * j + 32, 6, off:CH], vg[u][:, kb, j, :], pt[:, s % 3, j, off:CH],
                              start=(kb == 0), stop=(kb == 4 * c + 3))
                last.then_inc(av_done, 1)

            def run(g, k, u, first=False, last=False):
                for s, (c, kb, off, diag) in enumerate(KSTEPS):
                    if s == 0:
                        pe.wait_ge(rows_in[0], 16 * (g + 1))
                    if s == 4:
                        pe.wait_ge(rows_in[1], 16 * (g + 1))
                    for jj in range(2):
                        if not (first and s == 0):
                            pe.wait_ge(e_exped, g * EUNITS + 2 * s + jj - 1)
                        for j in (2 * jj, 2 * jj + 1):
                            ins = mm(ps[:, j, off:CH], kst[u][0:EROWS, j, kb * P:(kb + 1) * P], qst[u][0:EROWS, c, j, off:CH],
                                     start=True, stop=True)
                        ins.then_inc(e_scored, 1)
                    if s >= LAG:
                        values(g, u, s - LAG, first)
                    elif not first:
                        values(g - 1, 1 - u, STEPS + s - LAG)
                    if s == 1:
                        if first:
                            pe.wait_ge(m_rows_ready, 1)
                        else:
                            pe.wait_ge(turned, 2 * g - 1)
                        row_copy(g, 1)
                    if s == BACK1_STEP and not first:
                        pe.wait_ge(m_rows_ready, 2 * g + 2)
                        back(g - 1, 1)
                    if s == MROWS_STEP and not last:
                        if first:
                            pe.wait_ge(m_rows_ready, 2)
                        else:
                            pe.wait_ge(turned, 2 * g)
                        row_copy(g + 1, 0)
                    if s == BACK0_STEP:
                        if last:
                            pe.wait_ge(turned, 2 * g)
                        else:
                            pe.wait_ge(m_rows_ready, 2 * g + 3)
                        back(g, 0)
                    if not last:
                        if s == 0:
                            pe.wait_ge(stack_in[1 - u], 16 * 18 * (k + 1 + u))
                        for n in units_of_step(s):
                            max_unit(g + 1, 1 - u, n)

            pe.wait_ge(stack_in[0], 16 * 18)
            for n in range(MUN):
                max_unit(0, 0, n, first=True)
                if n == MUN_A + 4:
                    row_copy(0, 0)
            run(0, 0, 0, first=True)
            with pe.Fori(0, 3) as i:
                run(2 * i + 1, i, 1)
                run(2 * i + 2, i + 1, 0)
            run(7, 3, 1, last=True)
            for s in range(STEPS - LAG, STEPS):
                values(7, 1, s)
            pe.wait_ge(turned, 2 * NG - 1)
            back(7, 1)

            pe.wait_ge(turned, 2 * NG)
            for c in range(4):
                if c >= 2:
                    pe.wait_ge(aoT_ready, c - 1)
                for i in range(4):
                    t = 4 * c + i
                    b, qi = t // TB, t % TB
                    last = turn(ps[:, c % 2, i * P:(i + 1) * P], ao[:, qi, b * D:(b + 1) * D])
                last.then_inc(aoT_done, 1)
            for t in range(NT):
                pe.wait_ge(aoT_ready, t // 4 + 1)
                if t >= 2:
                    pe.wait_ge(x2_ready, t - 1)
                mm(ps[:, 2 + t % 2, 0:ZW], tT[:, t * P:(t + 1) * P], W("wo", ZM, D), start=True, stop=True).then_inc(proj_done, 1)
            for c in range(4):
                if c >= 2:
                    pe.wait_ge(xfT_ready, c - 1)
                for i in range(4):
                    t = 4 * c + i
                    pe.wait_ge(xf_ready, t + 1)
                    last = turn(ps[:, c % 2, i * P:(i + 1) * P], tmp[:, t, :])
                last.then_inc(xfT_done, 1)
            for t in range(NT):
                pe.wait_ge(xfT_ready, t // 4 + 1)
                last = mm(ps[:, 6, t * E:(t + 1) * E], tT[:, t * P:(t + 1) * P], W("gate"), start=True, stop=True)
            last.then_inc(gate_done, 1)
            for c in range(4):
                r = tT[:, c * CH:(c + 1) * CH]
                for i, (name, wn, nr, hb, src) in enumerate(MOE):
                    n = c * NB + i
                    if n >= 6:
                        pe.wait_ge(hb_read, n - 5)
                        pi = (n - 6) % NB
                        if MOE[pi][0] == "z1":
                            pe.wait_ge(glu_ready, 4 * ((n - 6) // NB) + MOE[pi][3] + 1)
                    if src:
                        pe.wait_ge(hb_read, c * NB + ORDER[(src, nr - 1)] + 1)
                    for q in range(nr):
                        if nr == 1:
                            wt, rr = W(wn, hb * P, (hb + 1) * P), (hid[:, SLOT[(src, 0)], :] if src else r)
                        else:
                            wt, rr = V(wn, q, hb * P, (hb + 1) * P), hid[:, SLOT[(src, q)], :]
                        ins = mm(ps[:, n % 6, :], wt, rr, start=(q == 0), stop=(q == nr - 1))
                    ins.then_inc(hb_done, 1)
                pe.wait_ge(glu_ready, 4 * (c + 1))
                pe.wait_ge(hb_read, NB * (c + 1))
                for t in range(4 * c, 4 * c + 4):
                    if t < 2:
                        pe.wait_ge(gmax_ready, 1)
                    else:
                        pe.wait_ge(out_ready, t - 1)
                    cc = (t % 4) * P
                    for e, (hn, wn) in enumerate((("h0", "e0_down"), ("z1", "e1_down"), ("a3", "e2_l4"), ("u3", "e3_out"))):
                        for q in range(2):
                            ins = mm(ps[:, 6 + t % 2, e * ZW:(e + 1) * ZW], hid[:, SLOT[(hn, q)], cc:cc + P], V(wn, q, ZM, D),
                                     start=(q == 0), stop=(q == 1))
                    ins.then_inc(down_done, 1)


_A = ("Wq", "Wk", "Wv", "Wo")


def kernel(**inputs):
    import numpy as np
    import concourse.bacc as bacc
    from concourse.bass_utils import run_bass_kernel_spmd

    def a(n):
        return np.asarray(inputs["L0_attn_" + n])

    def f(n):
        return np.asarray(inputs["L0_ffn_" + n])

    arrays = {
        "x": np.ascontiguousarray(a("summaries")),
        "wts": np.ascontiguousarray(np.concatenate(
            [a(n) for n in _A] + [f(n).T for n in ("wq", "wk", "wv", "wo", "gate_w", "e0_up", "e1_w1", "e1_w2", "e2_l1", "e3_down", "e3_up")], axis=1)),
        "wts2": np.ascontiguousarray(np.concatenate(
            [f(n).T for n in ("e0_down", "e1_down", "e2_l2", "e2_l3", "e2_l4", "e3_out")], axis=1)),
        "cols": np.ascontiguousarray(np.stack([a("bq"), a("bk"), f("n1_w"), f("n2_w")], axis=1)),
        "rows": np.ascontiguousarray(np.concatenate([a("bv"), a("bo"), f("qn_w"), f("kn_w")])[None]),
    }
    nc = bacc.Bacc("TRN2", target_bir_lowering=False, num_devices=1)
    args = [nc.dram_tensor("in_" + n, v.shape, mybir.dt.from_np(v.dtype), kind="ExternalInput").ap() for n, v in arrays.items()]
    args.append(nc.dram_tensor("out", (B, T, D), F32, kind="ExternalOutput").ap())
    build(nc, *args)
    r = run_bass_kernel_spmd(nc, [{"in_" + n: v for n, v in arrays.items()}], core_ids=[0])
    return r.results[0]["out"]
```

```python
from contextlib import ExitStack

import concourse.bass as bass
from concourse import mybir

F32 = mybir.dt.float32
BF16 = mybir.dt.bfloat16
U32 = mybir.dt.uint32
I32 = mybir.dt.int32
ALU = mybir.AluOpType
ACT = mybir.ActivationFunctionType
AX_X = mybir.AxisListType.X

P = 128
B, T, D = 2, 1024, 128
NT = B * T // P
TB = T // P
TOPK = 8
H, HD = 16, 8
HG = 4
NG = B * H // HG
CH = 512
HID = 256
E = 4
ZM = 32
ZW = D - ZM
NEG = -1.0e30
MARK = -3.0e38
FMAX = 3.4028234663852886e38
LN_EPS = 1e-5
RMS_EPS = 1.1920929e-07
ROWS = 48
PADR = 96
MROW = 96
EROWS = MROW + 3
Q_PARTS = (0, 0, 0, 1, 1, 2)
K_PARTS = (0, 1, 2, 0, 1, 0)
NBUF = 3
STACK_DMAS = 16 * 18
LAG = 2
STEPS = 12
EUNITS = 2 * STEPS
DIAGS = 16

W_COLS = {}
_at = 0
for _name, _n in (("Wq", D), ("Wk", D), ("Wv", D), ("Wo", D), ("qkv", 3 * D), ("wo", D), ("gate", E),
                  ("e0_up", HID), ("e1_w1", HID), ("e1_w2", HID), ("e2_l1", HID), ("e3_down", D), ("e3_up", HID)):
    W_COLS[_name] = (_at, _n)
    _at += _n
W_ALL = _at
W_ATT = 4 * D
V_COLS = {}
_at = 0
for _name, _n in (("e0_down", D), ("e1_down", D), ("e2_l2", HID), ("e2_l3", HID), ("e2_l4", D), ("e3_out", D)):
    V_COLS[_name] = (_at, _n)
    _at += _n
V_ALL = _at


def key_block_steps():
    out = []
    for c in range(2):
        for kb in range(4 * c + 4):
            diag = kb >= 4 * c
            out.append((c, kb, (kb - 4 * c) * P if diag else 0, diag))
    return out


def max_units():
    out = []
    for qi in range(TB):
        if qi >= 4:
            out += [(qi, j, 1, 0, CH, False) for j in range(HG)]
        w = P * (qi % 4 + 1)
        n = max(1, min(HG, CH // w)) if w != 3 * P else 1
        out += [(qi, j, n, CH * (qi // 4), w, True) for j in range(0, HG, n)]
    return out


KSTEPS = key_block_steps()
MUNITS = max_units()
MUN = len(MUNITS)
MUN_A = sum(u[0] < 4 for u in MUNITS)


def units_of_step(s):
    cols = [CH - k[2] for k in KSTEPS]
    return range(MUN * sum(cols[:s]) // sum(cols), MUN * sum(cols[:s + 1]) // sum(cols))


def order_of_step(s, more):
    out = [("e", 0), ("e", 1), ("v", None)]
    units = [("m", n) for n in units_of_step(s)] if more else []
    at = [0, 1, 2, 3]
    for i, m in reversed(list(enumerate(units))):
        out.insert(at[i * 4 // len(units)], m)
    return out


STEP_A = next(s for s in range(STEPS) if units_of_step(s).stop >= MUN_A)
MROWS_STEP = STEP_A + 2
BACK0_STEP = 8
BACK1_STEP = 3


LAST_A = NT + 4
LANE = {w: [] for w in range(40)}
for _w, _items in {
    0: [("xT", 2), ("q", 2)], 1: [("k", 2), ("v", 2)], 2: [("xT", 3), ("q", 3)], 3: [("k", 3), ("v", 3)],
    13: [("hT", 0), ("hT", 1), ("qkv", 0)], 14: [("qkv", 1), ("qkv", 2), ("qkv", 3)],
    15: [("qkv", 4), ("qkv", 5)], 16: [("qkv", 6), ("qkv", 7)],
    18: [("sp", 0)], 19: [("sp", 1), ("sp", 2)],
    20: [("sp", 3), ("sp", 4), ("sp", 5)],
    21: [("hT", 2), ("hT", 3), ("qkv", 8), ("qkv", 9), ("qkv", 10), ("qkv", 11)],
    22: [("qkv", 12), ("qkv", 13), ("qkv", 14), ("qkv", 15)],
    25: [("sp", 6), ("sp", 7), ("sp", 8)], 26: [("sp", 9), ("sp", 10), ("sp", 11)],
}.items():
    LANE[_w] = _items
NORM_SLOT = (12, 20)
QK_SLOT = (14, 16, 21, 22)
FRONT = 28
M0_SLOTS = range(22, 28)


def lane_bank(item):
    kind, n = item
    if kind in ("hT", "qkv", "sp") and n >= {"hT": 2, "qkv": 8, "sp": 3}[kind]:
        return {"hT": n % 2, "qkv": 2 + n % 2, "sp": n % 2}[kind]
    return 7


def lane_before():
    last, out = {7: ("v", 1)}, {}
    for w in sorted(LANE):
        for item in LANE[w]:
            b = lane_bank(item)
            out[item] = last.get(b)
            last[b] = item
    return out


LANE_BEFORE = lane_before()


def m0_units(w):
    k, n = w - M0_SLOTS.start, len(M0_SLOTS)
    return range(MUN * k // n, MUN * (k + 1) // n)


def build(nc, x, wts, wts2, cols, rows, out):
    ctx = ExitStack()
    with ctx:
        def sb(name, shape, dt=F32):
            return ctx.enter_context(nc.sbuf_tensor(name, shape, dt))

        def sem(name):
            return ctx.enter_context(nc.semaphore(name))

        ps = ctx.enter_context(nc.psum_tensor("ps", [P, 8, CH], F32))
        ident = sb("ident", [P, P])
        identb = sb("identb", [P, P], BF16)
        maskb = sb("maskb", [P, P], BF16)
        w = sb("w", [P, W_ALL])
        w2 = sb("w2", [P, 2, V_ALL])
        col = sb("col", [P, 4])
        row = sb("row", [P, 2 * D + 2 * HD])
        xs = sb("xs", [P, NT, D])
        ys = sb("ys", [P, NT, D])
        tmp = sb("tmp", [P, NT, D])
        tT = sb("tT", [P, NT * P])
        st = sb("st", [P, NT, 6])
        mv = sb("mv", [P, NT, 2])
        sm = sb("sm", [P, 8, NT])
        AR = 2 * 2048 * NBUF + 6144
        ar = sb("ar", [P, AR])
        qT = ar[:, 0:2048]
        kT = ar[:, 2048:4096]
        vv = ar[:, 4096:6144].rearrange("p (t d) -> p t d", t=NT)
        prob = ar[:, 6144:8192].rearrange("p (n k) -> p n k", n=2)
        repl = ar[:, 8192:10240].rearrange("p (n k) -> p n k", n=2)
        psel = ar[:, 10240:12288].rearrange("p (n k) -> p n k", n=2)
        pselT = ar[:, 12288:14336].rearrange("p (n k) -> p n k", n=2)
        qst = [ar[:, 4096 * u:4096 * u + 2048].bitcast(BF16).rearrange("p (c j t) -> p c j t", c=2, j=HG) for u in range(NBUF)]
        kst = [ar[:, 4096 * u + 2048:4096 * u + 4096].bitcast(BF16).rearrange("p (j t) -> p j t", j=HG) for u in range(NBUF)]
        pt = ar[:, 4096 * NBUF:AR].rearrange("p (n j t) -> p n j t", n=3, j=HG)
        hid = ar[:, 0:28 * CH].rearrange("p (n t) -> p n t", n=28)
        qk = sb("qk", [P, 2, 4, 2 * D])
        sq = sb("sq", [P, 4, 2 * D])
        hs = sb("hs", [P, 3, 4 * 2 * H])
        parts = sb("parts", [P, 2, 3, 4, 2 * D], BF16)
        partT = sb("partT", [P, 3, 2, CH], BF16)
        va = sb("va", [P, NG, TB, HG * HD])
        vg = [sb(f"vg{u}", [P, TB, HG, 32]) for u in range(NBUF)]
        ao = sb("ao", [P, TB, B * D])
        avs = sb("avs", [P, 2, CH])
        rec = sb("rec", [P, 2, 4, HG])
        mxa = sb("mxa", [P, 3, HG, 4])
        mxm = sb("mxm", [P, 2, HG * 4])
        mxp = sb("mxp", [P, 2, 8, HG * 4], BF16)
        mxT = sb("mxT", [P, 2, P], BF16)
        m8 = sb("m8", [P, NT, 8])
        negm = sb("negm", [P, NT])
        den = sb("den", [P, NT])
        rden = sb("rden", [P, NT])
        aT = sb("aT", [P, 2, P])
        gl = sb("gl", [P, 10, NT, E])
        ga = sb("ga", [P, 4, NT])

        split = nc.dram_tensor("split", [6, B * D, T], BF16, kind="Internal").ap()

        def W(name, a=0, b=None):
            o, n = W_COLS[name]
            return w[:, o + a:o + (n if b is None else b)]

        def V(name, r, a=0, b=None):
            o, n = V_COLS[name]
            return w2[:, r, o + a:o + (n if b is None else b)]

        x_in = [sem(f"x_in{b}") for b in range(B)]
        wa_in = sem("wa_in")
        wf_in = sem("wf_in")
        vec_in = sem("vec_in")
        const_ready = sem("const_ready")
        y_scale_ready = sem("y_scale_ready")
        y_ready = sem("y_ready")
        xn_ready = sem("xn_ready")
        tr_done = sem("tr_done")
        tT_ready = sem("tT_ready")
        q_done = sem("q_done")
        k_done = sem("k_done")
        v_done = sem("v_done")
        q_ready = sem("q_ready")
        k_ready = sem("k_ready")
        v_ready = sem("v_ready")
        scored = sem("scored")
        chosen = sem("chosen")
        exped = sem("exped")
        psel_ready = sem("psel_ready")
        pT_done = sem("pT_done")
        pT_ready = sem("pT_ready")
        av_a = sem("av_a")
        aT_ready = sem("aT_ready")
        wo_done = sem("wo_done")
        x1_ready = sem("x1_ready")
        x1_stats = sem("x1_stats")
        vstep = sem("vstep")
        hT_done = sem("hT_done")
        hT_ready = sem("hT_ready")
        qkv_done = sem("qkv_done")
        qkv_read = sem("qkv_read")
        sq_ready = sem("sq_ready")
        ms_ready = sem("ms_ready")
        qk_scaled = sem("qk_scaled")
        qk_normed = sem("qk_normed")
        hi_ready = sem("hi_ready")
        r1_ready = sem("r1_ready")
        mid_ready = sem("mid_ready")
        lo_ready = sem("lo_ready")
        spT_done = sem("spT_done")
        spT_ready = sem("spT_ready")
        spT_stored = [sem(f"spT_stored{p}") for p in range(3)]
        pad_zero = sem("pad_zero")
        pads_ready = sem("pads_ready")
        stack_in = [sem(f"stack_in{u}") for u in range(NBUF)]
        m_scored = sem("m_scored")
        m_reduced = sem("m_reduced")
        max_step = sem("max_step")
        m_parts = sem("m_parts")
        m_rows_done = sem("m_rows_done")
        m_rows_ready = sem("m_rows_ready")
        rows_in = [sem(f"rows_in{h}") for h in range(2)]
        turned = sem("turned")
        e_scored = sem("e_scored")
        e_exped = sem("e_exped")
        unit_taken = sem("unit_taken")
        diag_done = sem("diag_done")
        vg_ready = sem("vg_ready")
        av_done = sem("av_done")
        avs_ready = sem("avs_ready")
        back_done = sem("back_done")
        norm_step = sem("norm_step")
        aoT_done = sem("aoT_done")
        aoT_ready = sem("aoT_ready")
        proj_done = sem("proj_done")
        x2_ready = sem("x2_ready")
        xf_ready = sem("xf_ready")
        xfT_done = sem("xfT_done")
        xfT_ready = sem("xfT_ready")
        gate_done = sem("gate_done")
        gate_exp = sem("gate_exp")
        gmax_ready = sem("gmax_ready")
        hb_done = sem("hb_done")
        hb_read = sem("hb_read")
        glu_ready = sem("glu_ready")
        down_done = sem("down_done")
        out_ready = sem("out_ready")
        out_sent = sem("out_sent")

        block = ctx.enter_context(nc.Block())

        MOE = []
        for hb in range(2):
            MOE.append(("h0", "e0_up", 1, hb, None))
        for hb in range(2):
            MOE.append(("a1", "e2_l1", 1, hb, None))
        for hb in range(2):
            MOE.append(("z1", "e1_w1", 1, hb, None))
        MOE.append(("d3", "e3_down", 1, 0, None))
        for hb in range(2):
            MOE.append(("a2", "e2_l2", 2, hb, "a1"))
        for hb in range(2):
            MOE.append(("z2", "e1_w2", 1, hb, None))
        for hb in range(2):
            MOE.append(("u3", "e3_up", 1, hb, "d3"))
        for hb in range(2):
            MOE.append(("a3", "e2_l3", 2, hb, "a2"))
        NB = len(MOE)
        SLOT = {}
        for name, _, _, hb, _ in MOE:
            SLOT[(name, hb)] = len(SLOT)
        ORDER = {(m[0], m[3]): i for i, m in enumerate(MOE)}

        @block.sync
        def _(sp):
            xt = x.rearrange("b (t p) d -> p (b t) d", p=P)
            for b in range(B):
                sp.dma_start(xs[:, b * TB:(b + 1) * TB, :], xt[:, b * TB:(b + 1) * TB, :]).then_inc(x_in[b], 16)

            def load_stacks(g, u):
                src = split[:, bass.ds(g * 32, 32), :]
                for p in range(6):
                    one = src[Q_PARTS[p]].rearrange("(j d) (c t) -> d c j t", d=HD, c=2)
                    for c in range(2):
                        sp.dma_start(qst[u][8 * p:8 * p + 8, c], one[:, c]).then_inc(stack_in[u], 16)
                    one = src[3 + K_PARTS[p]].rearrange("(j d) t -> d j t", d=HD)
                    sp.dma_start(kst[u][8 * p:8 * p + 8], one).then_inc(stack_in[u], 16)

            def load_rows(g, u, h):
                sp.wait_ge(m_rows_ready, 2 * g + h + 1)
                sp.dma_start(qst[u][MROW:MROW + 3, h].rearrange("p j (i t) -> p (j i) t", i=4),
                             mxT[0:48, h, :]).then_inc(rows_in[h], 16)

            def run(g, u, more, first=False, last=False):
                if more:
                    if not first:
                        sp.wait_ge(e_scored, g * EUNITS)
                    load_stacks(g + 2, (u + 2) % NBUF)
                load_rows(g, u, 1)
                if not last:
                    load_rows(g + 1, (u + 1) % NBUF, 0)

            for p in range(3):
                sp.wait_ge(spT_stored[p], 16 * 2)
            for u in range(2):
                sp.wait_ge(pads_ready, u + 1)
                load_stacks(u, u)
            load_rows(0, 0, 0)
            sp.wait_ge(pads_ready, NBUF)
            for g in range(NG):
                if g == 2:
                    for p in range(3):
                        sp.wait_ge(spT_stored[p], 16 * 4)
                run(g, g % NBUF, g < NG - 2, first=(g == 0), last=(g == NG - 1))
            ot = out.rearrange("b (t p) d -> p (b t) d", p=P)
            for c in range(4):
                sp.wait_ge(out_ready, 4 * (c + 1))
                sp.dma_start(ot[:, 4 * c:4 * c + 4, :], xs[:, 4 * c:4 * c + 4, :]).then_inc(out_sent, 16)
            sp.wait_ge(out_sent, 64)

        @block.gpsimd
        def _(pool):
            pool.memset(ident[:], 0.0).then_inc(const_ready, 1)
            pool.memset(identb[:], 0.0).then_inc(const_ready, 1)
            pool.memset(maskb[:], 0.0).then_inc(const_ready, 1)
            pool.wait_ge(const_ready, 3)
            for m in (ident, identb):
                pool.affine_select(out=m[:], in_=m[:], compare_op=ALU.not_equal, fill=1.0, base=0,
                                   pattern=[[-1, P]], channel_multiplier=1).then_inc(const_ready, 1)
            pool.affine_select(out=maskb[:], in_=maskb[:], compare_op=ALU.is_ge, fill=NEG, base=0,
                               pattern=[[-1, P]], channel_multiplier=1).then_inc(const_ready, 1)
            for u in range(NBUF):
                pool.memset(vg[u][:], 0.0).then_inc(const_ready, 1)
            pool.memset(mxp[:], 0.0)
            pool.wait_ge(const_ready, 9)
            for u in range(NBUF):
                pool.memset(vg[u][:, :, :, HD:HD + 1], 1.0).then_inc(const_ready, 1)

            def zero_pads(u):
                if u == 0:
                    pool.wait_ge(x1_ready, NT)
                pool.memset(ar[:, 4096 * u:4096 * u + 4096], 0.0).then_inc(pad_zero, 1)
                pool.wait_ge(pad_zero, u + 1)
                pool.memset(kst[u][MROW:MROW + 3], 1.0).then_inc(pads_ready, 1)
                pool.wait_ge(pads_ready, u + 1)

            pool.wait_ge(vec_in, 32)
            for z in range(4):
                pool.wait_ge(qkv_read, 4 * (z + 1))
                if z:
                    pool.wait_ge(ms_ready, z)
                pool.tensor_tensor(sq[:], qk[:, z % 2], qk[:, z % 2], ALU.mult).then_inc(sq_ready, 1)
                if z == 2:
                    zero_pads(0)
                pool.wait_ge(qk_scaled, z + 1)
                for s in range(2):
                    v = qk[:, z % 2, :, s * D:(s + 1) * D].rearrange("p t (h d) -> p t h d", h=H)
                    nw = row[:, 2 * D + s * HD:2 * D + (s + 1) * HD].unsqueeze(1).unsqueeze(1).to_broadcast([P, 4, H, HD])
                    pool.tensor_tensor(v, v, nw, ALU.mult).then_inc(qk_normed, 1)
            for u in range(1, NBUF):
                zero_pads(u)

            def copy_v(g, u):
                pool.tensor_copy(vg[u][:, :, :, 0:HD],
                                 va[:, bass.ds(g, 1)].rearrange("p o k (j d) -> p (o k) j d", j=HG)).then_inc(vg_ready, 1)

            pool.wait_ge(qkv_read, NT)
            copy_v(0, 0)

            def run(g, u, first=False, last=False):
                for s, (c, kb, off, diag) in enumerate(KSTEPS):
                    if diag:
                        for jj in range(2):
                            pool.wait_ge(e_exped, g * EUNITS + 2 * s + jj + 1)
                            pool.sem_inc(unit_taken, 1)
                            v = pt[:, s % 3, 2 * jj:2 * jj + 2, off:off + P]
                            pool.affine_select(out=v, in_=v, compare_op=ALU.is_ge, fill=0.0, base=0,
                                               pattern=[[0, 2], [1, P]], channel_multiplier=-1).then_inc(diag_done, 1)
                    if s == 4 and not last:
                        if not first:
                            pool.wait_ge(av_done, (g - 1) * STEPS + 1)
                        copy_v(g + 1, (u + 1) % NBUF)

            run(0, 0, first=True)
            with pool.Fori(0, 2) as i:
                run(3 * i + 1, 1)
                run(3 * i + 2, 2)
                run(3 * i + 3, 0)
            run(7, 1, last=True)

        @block.scalar
        def _(act):
            act.dma_start(w[:, 0:W_ATT], wts[:, 0:W_ATT]).then_inc(wa_in, 16)
            act.dma_start(col[:], cols).then_inc(vec_in, 16)
            act.dma_start(row[:], rows.to_broadcast([P, 2 * D + 2 * HD])).then_inc(vec_in, 16)
            act.dma_start(w[:, W_ATT:W_ALL], wts[:, W_ATT:W_ALL]).then_inc(wf_in, 16)
            act.dma_start(w2[:], wts2.rearrange("(r p) n -> p r n", p=P)).then_inc(wf_in, 16)
            act.wait_ge(vec_in, 32)
            def lane(item):
                kind, n = item
                bank = ps[:, lane_bank(item), :]
                cols_ = slice(n * CH, (n + 1) * CH)
                if kind == "xT":
                    act.wait_ge(tr_done, n + 1)
                    nc.scalar.copy(tT[:, cols_], bank).then_inc(tT_ready, 1)
                elif kind == "q":
                    act.wait_ge(q_done, n + 1)
                    nc.scalar.activation(qT[:, cols_], bank, ACT.Identity, bias=col[:, 0:1]).then_inc(q_ready, 1)
                elif kind == "hT":
                    act.wait_ge(hT_done, n + 1)
                    nc.scalar.activation(tT[:, cols_], bank, ACT.Copy, scale=col[:, 2:3]).then_inc(hT_ready, 1)
                elif kind == "qkv":
                    z = n // 4
                    act.wait_ge(qkv_done, n + 1)
                    if n % 4 == 0 and z >= 2:
                        act.wait_ge(lo_ready, z - 1)
                    nc.scalar.copy(qk[:, z % 2, n % 4, :], bank[:, 0:2 * D])
                    nc.scalar.copy(va[:, 4 * (n // TB):4 * (n // TB) + 4, n % TB, :],
                                   bank[:, 2 * D:3 * D].rearrange("p (g d) -> p g d", g=4)).then_inc(qkv_read, 1)
                elif kind == "sp":
                    z, p = n // 3, n % 3
                    act.wait_ge(spT_done, n + 1)
                    if z:
                        act.wait_ge(spT_stored[p], 16 * z)
                    nc.scalar.copy(partT[:, p].rearrange("p s t -> p (s t)"), bank.bitcast(BF16)).then_inc(spT_ready, 1)
                    act.wait_ge(spT_ready, n + 1)
                    b, q = z // 2, z % 2
                    act.dma_start(split.rearrange("(s q) f t -> q f s t", s=2)[p][b * D:(b + 1) * D, :, q * CH:(q + 1) * CH],
                                  partT[:, p]).then_inc(spT_stored[p], 16)

            for c in range(2):
                act.wait_ge(tr_done, c + 1)
                nc.scalar.copy(tT[:, c * CH:(c + 1) * CH], ps[:, c, :]).then_inc(tT_ready, 1)
            for c in range(2):
                act.wait_ge(q_done, c + 1)
                nc.scalar.activation(qT[:, c * CH:(c + 1) * CH], ps[:, 2 + c, :], ACT.Identity,
                                     bias=col[:, 0:1]).then_inc(q_ready, 1)
            for t in range(FRONT):
                lanes = LANE[t] + [None] * 3
                if lanes[0]:
                    lane(lanes[0])
                if 3 <= t < NT + 3:
                    n = t - 3
                    act.wait_ge(av_a, n + 1)
                    if n >= 2:
                        act.wait_ge(wo_done, n - 1)
                    nc.scalar.copy(aT[:, n % 2, :], ps[:, 6, 0:P]).then_inc(aT_ready, 1)
                if lanes[1]:
                    lane(lanes[1])
                if t < NT:
                    wdt = P * (t % TB + 1)
                    act.wait_ge(chosen, t + 1)
                    if t >= 2:
                        act.wait_ge(psel_ready, t - 1)
                    nc.scalar.activation(prob[:, t % 2, 0:wdt], ps[:, 2 * (t % 2):2 * (t % 2) + 2, :].rearrange("p a b -> p (a b)")[:, 0:wdt],
                                         ACT.Exp, bias=negm[:, t:t + 1], scale=float(D) ** -0.5).then_inc(exped, 1)
                if 2 <= t < NT + 2:
                    n = t - 2
                    wdt = P * (n % TB + 1)
                    act.wait_ge(pT_done, n + 1)
                    if n >= 2:
                        act.wait_ge(av_a, n - 1)
                    nc.scalar.copy(pselT[:, n % 2, 0:wdt], ps[:, 4:6, :].rearrange("p a b -> p (a b)")[:, 0:wdt]).then_inc(pT_ready, 1)
                for item in lanes[2:]:
                    if item:
                        lane(item)
                if t in NORM_SLOT:
                    b = NORM_SLOT.index(t)
                    act.wait_ge(y_scale_ready, b + 1)
                    for n in range(b * TB, (b + 1) * TB):
                        nc.scalar.activation(ys[:, n, :], xs[:, n, :], ACT.Identity, bias=sm[:, 3, n:n + 1],
                                             scale=sm[:, 4, n:n + 1]).then_inc(y_ready, 1)
                for z in range(4):
                    if t == QK_SLOT[z] + 2:
                        act.wait_ge(qk_normed, 2 * (z + 1))
                        if z >= 2:
                            act.wait_ge(spT_done, 3 * (z - 1))
                        nc.scalar.copy(parts[:, z % 2, 0], qk[:, z % 2]).then_inc(hi_ready, 1)
                    if t == QK_SLOT[z] + 3:
                        act.wait_ge(r1_ready, z + 1)
                        nc.scalar.copy(parts[:, z % 2, 1], qk[:, z % 2]).then_inc(mid_ready, 1)

            def row_copy(g, h, first=False):
                act.wait_ge(m_rows_done, 2 * g + h + 1)
                if not first:
                    act.wait_ge(rows_in[h], 16 * g)
                nc.scalar.copy(mxT[0:48, h, :], ps[0:48, 7, 0:64].bitcast(BF16)).then_inc(m_rows_ready, 1)

            def run(g, first=False, last=False):
                for s, (c, kb, off, diag) in enumerate(KSTEPS):
                    for jj in range(2):
                        act.wait_ge(e_scored, g * EUNITS + 2 * s + jj + 1)
                        if jj == 0 and not (first and s < 3):
                            act.wait_ge(av_done, g * STEPS + s - 2)
                        nc.scalar.activation(pt[:, s % 3, 2 * jj:2 * jj + 2, off:CH], ps[:, 2 * jj:2 * jj + 2, off:CH],
                                             ACT.Exp, scale=float(HD) ** -0.5).then_inc(e_exped, 1)
                    if s == 1:
                        row_copy(g, 1, first)
                    if s == MROWS_STEP and not last:
                        row_copy(g + 1, 0)

            row_copy(0, 0, first=True)
            run(0, first=True)
            with act.Fori(0, 2) as i:
                for k in (1, 2, 3):
                    run(3 * i + k)
            run(7, last=True)

            for c in range(4):
                act.wait_ge(aoT_done, c + 1)
                nc.scalar.copy(tT[:, c * CH:(c + 1) * CH], ps[:, c % 2, :]).then_inc(aoT_ready, 1)
            for c in range(4):
                act.wait_ge(xfT_done, c + 1)
                nc.scalar.activation(tT[:, c * CH:(c + 1) * CH], ps[:, c % 2, :], ACT.Copy, scale=col[:, 3:4]).then_inc(xfT_ready, 1)
            act.wait_ge(gmax_ready, 1)
            nc.scalar.activation(gl[:, 2], gl[:, 1], ACT.Exp).then_inc(gate_exp, 1)
            for c in range(4):
                for i, (name, wn, nr, hb, src) in enumerate(MOE):
                    n = c * NB + i
                    act.wait_ge(hb_done, n + 1)
                    if c and i == 0:
                        act.wait_ge(down_done, 4 * c)
                    o = hid[:, SLOT[(name, hb)], :]
                    bank = ps[:, n % 6, :]
                    if name == "z1":
                        nc.scalar.activation(o, bank, ACT.Tanh, scale=0.5).then_inc(hb_read, 1)
                    elif name == "z2":
                        nc.scalar.copy(o, bank).then_inc(hb_read, 1)
                    else:
                        nc.scalar.activation(o, bank, ACT.Gelu).then_inc(hb_read, 1)

        @block.vector
        def _(dve):
            v = nc.vector
            count = [0]

            def link(ins):
                count[0] += 1
                ins.then_inc(vstep, 1)
                dve.wait_ge(vstep, count[0])

            def rsqrt(y, val, scratch):
                link(v.tensor_scalar(y.bitcast(U32), val.bitcast(U32), 1, None, ALU.logical_shift_right))
                link(v.tensor_scalar(y.bitcast(I32), y.bitcast(I32), -1.0, float(0x5f3759df), ALU.mult, ALU.add))
                for _ in range(3):
                    link(v.tensor_tensor(scratch, y, y, ALU.mult))
                    link(v.scalar_tensor_tensor(out=scratch, in0=scratch, scalar=-0.5, in1=val, op0=ALU.mult, op1=ALU.mult))
                    link(v.scalar_tensor_tensor(out=y, in0=scratch, scalar=1.5, in1=y, op0=ALU.add, op1=ALU.mult))

            def stats(src, tiles):
                for t in tiles:
                    last = v.bn_stats(st[:, t, :], src[:, t, :])
                link(last)
                for t in tiles:
                    last = v.bn_aggr(mv[:, t, :], st[:, t, :])
                link(last)

            for b in range(B):
                dve.wait_ge(x_in[b], 16)
                tiles = range(b * TB, (b + 1) * TB)
                bt = slice(b * TB, (b + 1) * TB)
                stats(xs, tiles)
                link(v.tensor_scalar(sm[:, 0, bt], mv[:, bt, 1], LN_EPS, None, ALU.add))
                rsqrt(sm[:, 4, bt], sm[:, 0, bt], sm[:, 7, bt])
                for t in tiles:
                    v.tensor_scalar(tmp[:, t, :], xs[:, t, :], mv[:, t, 0:1], sm[:, 4, t:t + 1], ALU.subtract, ALU.mult).then_inc(xn_ready, 1)
            dve.wait_ge(vec_in, 32)

            def take_k(c, bank):
                dve.wait_ge(k_done, c + 1)
                v.tensor_scalar(kT[:, c * CH:(c + 1) * CH], ps[:, bank, :], col[:, 1:2], None, ALU.add).then_inc(k_ready, 1)

            def take_v(c, bank):
                dve.wait_ge(v_done, c + 1)
                v.tensor_tensor(vv[:, 4 * c:4 * c + 4, :], ps[:, bank, :].rearrange("p (t d) -> p t d", t=4),
                                row[:, 0:D].unsqueeze(1).to_broadcast([P, 4, D]), ALU.add).then_inc(v_ready, 1)

            for c in range(2):
                take_k(c, 4 + c)
                take_v(c, 6 + c)
            dve.wait_ge(xn_ready, NT)
            link(v.tensor_tensor(xs[:], xs[:], row[:, D:2 * D].unsqueeze(1).to_broadcast([P, NT, D]), ALU.add))

            def reduce_unit(g, n, first=False):
                qi, j, nh, k0, wdt, diag = MUNITS[n]
                if n == 0 and not first:
                    dve.wait_ge(max_step, 8 * g - 3)
                dve.wait_ge(m_scored, g * MUN + n + 1)
                which = 0 if qi < 4 else (2 if diag else 1)
                v.tensor_reduce(mxa[:, which, j:j + nh, qi % 4], ps[:, 4 + n % 2, 0:nh * wdt].rearrange("p (j k) -> p j k", j=nh),
                                AX_X, ALU.max).then_inc(m_reduced, 1)

            def split_maxima(g, h, first=False):
                a = mxa[:, 0 if h == 0 else 1].rearrange("p j i -> p (j i)")
                b = mxa[:, 0 if h == 0 else 2].rearrange("p j i -> p (j i)")
                base = (2 * g + h) * 4
                dve.wait_ge(m_reduced, g * MUN + (MUN_A if h == 0 else MUN))
                if not (first and h == 0):
                    dve.wait_ge(m_parts, 2 * g + h)
                v.tensor_tensor(mxm[:, 0], a, b, ALU.max).then_inc(max_step, 1)
                dve.wait_ge(max_step, base + 1)
                if not first:
                    dve.wait_ge(m_rows_done, 2 * g + h - 1)
                v.tensor_scalar(mxp[:, h, 0], mxm[:, 0], -1.0, None, ALU.mult).then_inc(max_step, 1)
                dve.wait_ge(max_step, base + 2)
                v.scalar_tensor_tensor(out=mxm[:, 1], in0=mxm[:, 0], scalar=-1.0, in1=mxp[:, h, 0],
                                       op0=ALU.mult, op1=ALU.subtract).then_inc(max_step, 1)
                dve.wait_ge(max_step, base + 3)
                v.tensor_copy(mxp[:, h, 1], mxm[:, 1]).then_inc(max_step, 1)
                dve.wait_ge(max_step, base + 4)
                v.tensor_tensor(mxp[:, h, 2], mxm[:, 1], mxp[:, h, 1], ALU.subtract).then_inc(m_parts, 1)

            def take_sums(g, c, first=False):
                dve.wait_ge(av_done, g * STEPS + (4 if c == 0 else STEPS))
                if not first:
                    dve.wait_ge(back_done, 2 * g + c)
                v.tensor_copy(avs[:, c, :], ps[:, 6, :]).then_inc(avs_ready, 1)

            def normalise(g, c, first=False):
                dve.wait_ge(back_done, 2 * g + c + 1)
                t4 = ps[:, 7, :].rearrange("p (i j d) -> p i j d", i=4, j=HG)
                if not first:
                    dve.wait_ge(turned, 2 * g + c)
                v.reciprocal(rec[:, c], t4[:, :, :, HD]).then_inc(norm_step, 1)
                dve.wait_ge(norm_step, 2 * g + c + 1)
                o = ao[:, 4 * c:4 * c + 4, bass.ds(g * HG * HD, HG * HD)].rearrange("p i (j d) -> p i j d", j=HG)
                v.tensor_tensor(o, t4[:, :, :, 0:HD], rec[:, c].unsqueeze(3).to_broadcast([P, 4, HG, HD]), ALU.mult).then_inc(turned, 1)

            def run(g, first=False, last=False):
                for s in range(STEPS):
                    if s == 2 and not first:
                        take_sums(g - 1, 1)
                    if s == BACK1_STEP + 1 and not first:
                        normalise(g - 1, 1)
                    if s == 4 + LAG:
                        take_sums(g, 0, first)
                    if s == BACK0_STEP + 1:
                        normalise(g, 0, first)
                    if not last:
                        for n in units_of_step(s):
                            reduce_unit(g + 1, n)
                        if s == STEP_A:
                            split_maxima(g + 1, 0)
                if not last:
                    split_maxima(g + 1, 1)

            def norm_x1(b):
                tiles = range(b * TB, (b + 1) * TB)
                bt = slice(b * TB, (b + 1) * TB)
                dve.wait_ge(x1_stats, (b + 1) * TB)
                for t in tiles:
                    last = v.bn_aggr(mv[:, t, :], st[:, t, :])
                link(last)
                link(v.tensor_scalar(sm[:, 0, bt], mv[:, bt, 1], LN_EPS, None, ALU.add))
                rsqrt(sm[:, 4, bt], sm[:, 0, bt], sm[:, 7, bt])
                v.scalar_tensor_tensor(out=sm[:, 3, bt], in0=mv[:, bt, 0], scalar=-1.0, in1=sm[:, 4, bt],
                                       op0=ALU.mult, op1=ALU.mult).then_inc(y_scale_ready, 1)
                link(v.tensor_tensor(sm[:, 2, bt], sm[:, 4, bt], sm[:, 4, bt], ALU.mult))
                link(v.tensor_tensor(sm[:, 2, bt], sm[:, 2, bt], mv[:, bt, 1], ALU.mult))
                link(v.tensor_scalar(sm[:, 2, bt], sm[:, 2, bt], RMS_EPS, None, ALU.add))
                rsqrt(sm[:, 5, bt], sm[:, 2, bt], sm[:, 7, bt])
                link(v.tensor_tensor(sm[:, 5, bt], sm[:, 5, bt], sm[:, 4, bt], ALU.mult))
                for t in tiles:
                    v.tensor_scalar(tmp[:, t, :], xs[:, t, :], mv[:, t, 0:1], sm[:, 5, t:t + 1], ALU.subtract, ALU.mult).then_inc(xn_ready, 1)

            for t in range(FRONT):
                if 4 <= t < NT + 4:
                    n = t - 4
                    dve.wait_ge(psel_ready, n + 1)
                    link(v.reciprocal(rden[:, n:n + 1], den[:, n:n + 1]))
                    dve.wait_ge(wo_done, n + 1)
                    v.scalar_tensor_tensor(out=xs[:, n, :], in0=ps[:, 6, 0:D], scalar=rden[:, n:n + 1], in1=xs[:, n, :],
                                           op0=ALU.mult, op1=ALU.add).then_inc(x1_ready, 1)
                for item in LANE[t]:
                    if item[0] == "k":
                        take_k(item[1], 7)
                    if item[0] == "v":
                        take_v(item[1], 7)
                if t < NT:
                    wdt = P * (t % TB + 1)
                    dve.wait_ge(scored, t + 1)
                    s = ps[:, 2 * (t % 2):2 * (t % 2) + 2, :].rearrange("p a b -> p (a b)")[:, 0:wdt]
                    link(v.max(m8[:, t, :], s))
                    if t >= 2:
                        dve.wait_ge(psel_ready, t - 1)
                    v.tensor_scalar(negm[:, t:t + 1], m8[:, t, 0:1], -float(D) ** -0.5, None, ALU.mult)
                    v.match_replace(out=repl[:, t % 2, 0:wdt], in_to_replace=m8[:, t, :], in_values=s, imm_value=MARK).then_inc(chosen, 1)
                if 4 <= t < NT + 4:
                    dve.wait_ge(x1_ready, n + 1)
                    v.bn_stats(st[:, n, :], xs[:, n, :]).then_inc(x1_stats, 1)
                if 1 <= t < NT + 1:
                    n = t - 1
                    wdt = P * (n % TB + 1)
                    dve.wait_ge(exped, n + 1)
                    if n >= 2:
                        dve.wait_ge(pT_done, n - 1)
                    v.scalar_tensor_tensor(out=psel[:, n % 2, 0:wdt], in0=repl[:, n % 2, 0:wdt], scalar=MARK, in1=prob[:, n % 2, 0:wdt],
                                           op0=ALU.is_equal, op1=ALU.mult, accum_out=den[:, n:n + 1]).then_inc(psel_ready, 1)
                if t in NORM_SLOT:
                    norm_x1(NORM_SLOT.index(t))
                for z in range(4):
                    one = qk[:, z % 2]
                    if t == QK_SLOT[z] + 4:
                        dve.wait_ge(mid_ready, z + 1)
                        v.tensor_tensor(parts[:, z % 2, 2], one, parts[:, z % 2, 1], ALU.subtract).then_inc(lo_ready, 1)
                    if t == QK_SLOT[z] + 3:
                        dve.wait_ge(hi_ready, z + 1)
                        v.tensor_tensor(one, one, parts[:, z % 2, 0], ALU.subtract).then_inc(r1_ready, 1)
                    if t == QK_SLOT[z] + 1:
                        dve.wait_ge(sq_ready, z + 1)
                        if z:
                            dve.wait_ge(qk_scaled, z)
                        link(v.tensor_reduce(hs[:, 1, :], sq[:].rearrange("p t (h d) -> p (t h) d", d=HD), AX_X, ALU.add))
                        v.tensor_scalar(hs[:, 0, :], hs[:, 1, :], 1.0 / HD, RMS_EPS, ALU.mult, ALU.add).then_inc(ms_ready, 1)
                        dve.wait_ge(ms_ready, z + 1)
                        rsqrt(hs[:, 1, :], hs[:, 0, :], hs[:, 2, :])
                        q4 = one.rearrange("p t (h d) -> p (t h) d", d=HD)
                        v.tensor_tensor(q4, q4, hs[:, 1, :].unsqueeze(2).to_broadcast([P, 8 * H, HD]), ALU.mult).then_inc(qk_scaled, 1)
                if t in M0_SLOTS:
                    for n in m0_units(t):
                        reduce_unit(0, n, first=True)
                        if n == MUN_A - 1:
                            split_maxima(0, 0, first=True)
            split_maxima(0, 1, first=True)

            run(0, first=True)
            with dve.Fori(0, 2) as i:
                for k in (1, 2, 3):
                    run(3 * i + k)
            run(7, last=True)
            take_sums(7, 1)
            normalise(7, 1)
            dve.wait_ge(turned, 2 * NG)

            dve.wait_ge(y_ready, NT)
            for t in range(NT):
                dve.wait_ge(proj_done, t + 1)
                v.tensor_tensor(ys[:, t, ZM:D], ys[:, t, ZM:D], ps[:, 2 + t % 2, 0:ZW], ALU.add).then_inc(x2_ready, 1)
            dve.wait_ge(x2_ready, NT)
            stats(ys, range(NT))
            link(v.tensor_tensor(sm[:, 2, :], mv[:, :, 0], mv[:, :, 0], ALU.mult))
            link(v.tensor_tensor(sm[:, 2, :], sm[:, 2, :], mv[:, :, 1], ALU.add))
            link(v.tensor_scalar(sm[:, 0, :], sm[:, 2, :], RMS_EPS, None, ALU.add))
            rsqrt(sm[:, 4, :], sm[:, 0, :], sm[:, 7, :])
            for t in range(NT):
                v.tensor_scalar(tmp[:, t, :], ys[:, t, :], sm[:, 4, t:t + 1], None, ALU.mult).then_inc(xf_ready, 1)
            link(v.tensor_tensor(xs[:], xs[:], ys[:], ALU.add))
            dve.wait_ge(gate_done, 1)
            raw, logit, num, prb, win, cmp_ = (gl[:, i] for i in range(6))
            link(v.tensor_copy(raw, ps[:, 6, 0:NT * E].rearrange("p (t e) -> p t e", t=NT)))
            link(v.tensor_tensor(cmp_, raw, raw, ALU.is_equal))
            link(v.memset(logit, 0.0))
            link(v.copy_predicated(logit, cmp_.bitcast(U32), raw))
            link(v.tensor_scalar(logit, logit, FMAX, -FMAX, ALU.min, ALU.max))
            link(v.tensor_reduce(ga[:, 0], logit, AX_X, ALU.max))
            v.tensor_tensor(logit, logit, ga[:, 0].unsqueeze(2).to_broadcast([P, NT, E]), ALU.subtract).then_inc(gmax_ready, 1)
            dve.wait_ge(gate_exp, 1)
            link(v.tensor_reduce(ga[:, 1], num, AX_X, ALU.add))
            link(v.reciprocal(ga[:, 2], ga[:, 1]))
            link(v.tensor_tensor(prb, num, ga[:, 2].unsqueeze(2).to_broadcast([P, NT, E]), ALU.mult))
            link(v.memset(win, 0.0))
            for a in range(E):
                for b in range(a + 1, E):
                    link(v.tensor_tensor(cmp_[:, :, 0], prb[:, :, a], prb[:, :, b], ALU.is_ge))
                    link(v.tensor_tensor(win[:, :, a], win[:, :, a], cmp_[:, :, 0], ALU.add))
                    link(v.scalar_tensor_tensor(out=win[:, :, b], in0=win[:, :, b], scalar=1.0, in1=cmp_[:, :, 0],
                                                op0=ALU.add, op1=ALU.subtract))
            link(v.scalar_tensor_tensor(out=prb, in0=win, scalar=2.0, in1=prb, op0=ALU.is_ge, op1=ALU.mult))
            link(v.tensor_reduce(ga[:, 1], prb, AX_X, ALU.add))
            link(v.tensor_scalar(ga[:, 1], ga[:, 1], 1e-8, None, ALU.add))
            link(v.reciprocal(ga[:, 2], ga[:, 1]))
            link(v.tensor_tensor(prb, prb, ga[:, 2].unsqueeze(2).to_broadcast([P, NT, E]), ALU.mult))

            for c in range(4):
                for hb in range(2):
                    t1 = hid[:, SLOT[("z1", hb)], :]
                    dve.wait_ge(hb_read, c * NB + ORDER[("z1", hb)] + 1)
                    v.scalar_tensor_tensor(out=t1, in0=t1, scalar=1.0, in1=ps[:, (c * NB + ORDER[("z1", hb)]) % 6, :],
                                           op0=ALU.add, op1=ALU.mult).then_inc(glu_ready, 1)
                for hb in range(2):
                    t1 = hid[:, SLOT[("z1", hb)], :]
                    dve.wait_ge(hb_read, c * NB + ORDER[("z2", hb)] + 1)
                    dve.wait_ge(glu_ready, 4 * c + hb + 1)
                    v.scalar_tensor_tensor(out=t1, in0=hid[:, SLOT[("z2", hb)], :], scalar=0.5, in1=t1,
                                           op0=ALU.mult, op1=ALU.mult).then_inc(glu_ready, 1)
                for t in range(4 * c, 4 * c + 4):
                    dve.wait_ge(down_done, t + 1)
                    for e in range(E):
                        ins = v.scalar_tensor_tensor(out=xs[:, t, ZM:D], in0=ps[:, 6 + t % 2, e * ZW:(e + 1) * ZW], scalar=prb[:, t, e:e + 1],
                                                     in1=xs[:, t, ZM:D], op0=ALU.mult, op1=ALU.add)
                        if e < E - 1:
                            link(ins)
                        else:
                            ins.then_inc(out_ready, 1)

        @block.tensor
        def _(pe):
            mm = nc.tensor.matmul

            def turn(dst, src):
                return nc.tensor.transpose(dst, src, ident[:])

            pe.wait_ge(const_ready, 12)
            def turn_tiles(bank, c, first):
                for i in range(4):
                    pe.wait_ge(xn_ready, first + 4 * c + i + 1)
                    last = turn(ps[:, bank, i * P:(i + 1) * P], tmp[:, 4 * c + i, :])
                return last

            def values_of(bank, c):
                for i in range(4):
                    t = 4 * c + i
                    last = mm(ps[:, bank, i * P:(i + 1) * P], tT[:, t * P:(t + 1) * P], W("Wv"), start=True, stop=True)
                return last

            for c in range(2):
                turn_tiles(c, c, 0).then_inc(tr_done, 1)
            pe.wait_ge(wa_in, 16)
            for c in range(2):
                pe.wait_ge(tT_ready, c + 1)
                r = tT[:, c * CH:(c + 1) * CH]
                mm(ps[:, 2 + c, :], W("Wq"), r, start=True, stop=True).then_inc(q_done, 1)
                mm(ps[:, 4 + c, :], W("Wk"), r, start=True, stop=True).then_inc(k_done, 1)
                values_of(6 + c, c).then_inc(v_done, 1)

            def lane(item):
                kind, n = item
                b = lane_bank(item)
                bank = ps[:, b, :]
                before = LANE_BEFORE[item]
                if before:
                    read = {"xT": tT_ready, "q": q_ready, "k": k_ready, "v": v_ready, "hT": hT_ready, "qkv": qkv_read, "sp": spT_ready}
                    pe.wait_ge(read[before[0]], before[1] + 1)
                if kind == "xT":
                    turn_tiles(b, n, 0).then_inc(tr_done, 1)
                elif kind == "q":
                    pe.wait_ge(tT_ready, n + 1)
                    mm(bank, W("Wq"), tT[:, n * CH:(n + 1) * CH], start=True, stop=True).then_inc(q_done, 1)
                elif kind == "k":
                    mm(bank, W("Wk"), tT[:, n * CH:(n + 1) * CH], start=True, stop=True).then_inc(k_done, 1)
                elif kind == "v":
                    values_of(b, n).then_inc(v_done, 1)
                elif kind == "hT":
                    turn_tiles(b, n, NT).then_inc(hT_done, 1)
                elif kind == "qkv":
                    if n == 0:
                        pe.wait_ge(wf_in, 32)
                    pe.wait_ge(hT_ready, n // 4 + 1)
                    mm(bank[:, 0:3 * D], tT[:, n * P:(n + 1) * P], W("qkv"), start=True, stop=True).then_inc(qkv_done, 1)
                elif kind == "sp":
                    z, p = n // 3, n % 3
                    pe.wait_ge((hi_ready, mid_ready, lo_ready)[p], z + 1)
                    bb = bank.bitcast(BF16)
                    for s in range(2):
                        for i in range(4):
                            last = nc.tensor.transpose(bb[:, s * CH + i * P:s * CH + (i + 1) * P],
                                                       parts[:, z % 2, p, i, s * D:(s + 1) * D], identb[:])
                    last.then_inc(spT_done, 1)

            def max_unit(g, u, n, first=False):
                qi, j, nh, k0, wdt, diag = MUNITS[n]
                if not (first and n < 2):
                    pe.wait_ge(m_reduced, g * MUN + n - 1)
                bank = ps[:, 4 + n % 2, :]
                for a in range(nh):
                    last = mm(bank[:, a * wdt:(a + 1) * wdt], qst[u][0:PADR, qi // 4, j + a, (qi % 4) * P:(qi % 4 + 1) * P],
                              kst[u][0:PADR, j + a, k0:k0 + wdt], start=True, stop=not diag)
                    if diag:
                        last = mm(bank[:, (a + 1) * wdt - P:(a + 1) * wdt], identb[:], maskb[:], start=False, stop=True)
                last.then_inc(m_scored, 1)

            def row_copy(g, h):
                pe.wait_ge(m_parts, 2 * g + h + 1)
                bank = ps[:, 7, 0:64].bitcast(BF16)
                nc.tensor.transpose(bank, mxp[:, h].rearrange("p a b -> p (a b)"), identb[:]).then_inc(m_rows_done, 1)

            def back(g, c):
                pe.wait_ge(avs_ready, 2 * g + c + 1)
                for i in range(4):
                    last = turn(ps[:, 7, i * P:(i + 1) * P], avs[:, c, i * P:(i + 1) * P])
                last.then_inc(back_done, 1)

            def values(g, u, s, first=False):
                c, kb, off, diag = KSTEPS[s]
                if kb == 0:
                    if not (first and c == 0):
                        pe.wait_ge(avs_ready, 2 * g + c)
                    if c == 0:
                        pe.wait_ge(vg_ready, g + 1)
                if diag:
                    nd = sum(KSTEPS[i][3] for i in range(s + 1))
                    pe.wait_ge(diag_done, g * DIAGS + 2 * nd)
                else:
                    pe.wait_ge(e_exped, g * EUNITS + 2 * s + 2)
                for j in range(HG):
                    last = mm(ps[32 * j:32 * j + 32, 6, off:CH], vg[u][:, kb, j, :], pt[:, s % 3, j, off:CH],
                              start=(kb == 0), stop=(kb == 4 * c + 3))
                last.then_inc(av_done, 1)

            def run(g, stacks_of_next, u, first=False, last=False):
                for s, (c, kb, off, diag) in enumerate(KSTEPS):
                    if s == 0:
                        pe.wait_ge(rows_in[0], 16 * (g + 1))
                    if s == 4:
                        pe.wait_ge(rows_in[1], 16 * (g + 1))
                    if s == 0 and not last:
                        pe.wait_ge(stack_in[(u + 1) % NBUF], stacks_of_next)
                    for what, n in order_of_step(s, not last):
                        if what == "m":
                            max_unit(g + 1, (u + 1) % NBUF, n)
                        elif what == "e":
                            if not (first and s == 0):
                                pe.wait_ge(e_exped, g * EUNITS + 2 * s + n - 1)
                            for j in (2 * n, 2 * n + 1):
                                ins = mm(ps[:, j, off:CH], kst[u][0:EROWS, j, kb * P:(kb + 1) * P], qst[u][0:EROWS, c, j, off:CH],
                                         start=True, stop=True)
                            ins.then_inc(e_scored, 1)
                        elif s >= LAG:
                            values(g, u, s - LAG, first)
                        elif not first:
                            values(g - 1, (u - 1) % NBUF, STEPS + s - LAG)
                    if s == 1:
                        if first:
                            pe.wait_ge(m_rows_ready, 1)
                        else:
                            pe.wait_ge(turned, 2 * g - 1)
                        row_copy(g, 1)
                    if s == BACK1_STEP and not first:
                        pe.wait_ge(m_rows_ready, 2 * g + 2)
                        back(g - 1, 1)
                    if s == MROWS_STEP and not last:
                        if first:
                            pe.wait_ge(m_rows_ready, 2)
                        else:
                            pe.wait_ge(turned, 2 * g)
                        row_copy(g + 1, 0)
                    if s == BACK0_STEP:
                        if last:
                            pe.wait_ge(turned, 2 * g)
                        else:
                            pe.wait_ge(m_rows_ready, 2 * g + 3)
                        back(g, 0)
            for t in range(FRONT):
                lanes = LANE[t] + [None] * 3
                if 4 <= t < NT + 4:
                    n = t - 4
                    pe.wait_ge(aT_ready, n + 1)
                    mm(ps[:, 6, 0:D], aT[:, n % 2, :], W("Wo"), start=True, stop=True).then_inc(wo_done, 1)
                if t < NT:
                    b, qi = t // TB, t % TB
                    if t in (0, TB):
                        for ready in (q_ready, k_ready, v_ready):
                            pe.wait_ge(ready, 2 * b + 2)
                    if t >= 2:
                        pe.wait_ge(exped, t - 1)
                    for k0 in range(0, P * (qi + 1), CH):
                        n = min(CH, P * (qi + 1) - k0)
                        bank = ps[:, 2 * (t % 2) + k0 // CH, :]
                        diag = k0 + n == P * (qi + 1)
                        last = mm(bank[:, 0:n], qT[:, t * P:(t + 1) * P], kT[:, b * T + k0:b * T + k0 + n], start=True, stop=not diag)
                        if diag:
                            last = mm(bank[:, n - P:n], identb[:], maskb[:], start=False, stop=True)
                    last.then_inc(scored, 1)
                if lanes[0]:
                    lane(lanes[0])
                if 3 <= t < NT + 3:
                    n = t - 3
                    pe.wait_ge(pT_ready, n + 1)
                    if n >= 1:
                        pe.wait_ge(x1_ready, n)
                    nk = n % TB + 1
                    for kb in range(nk):
                        last = mm(ps[:, 6, 0:P], vv[:, (n // TB) * TB + kb, :], pselT[:, n % 2, kb * P:(kb + 1) * P],
                                  start=(kb == 0), stop=(kb == nk - 1))
                    last.then_inc(av_a, 1)
                if lanes[1]:
                    lane(lanes[1])
                if 2 <= t < NT + 2:
                    n = t - 2
                    pe.wait_ge(psel_ready, n + 1)
                    if n >= 1:
                        pe.wait_ge(pT_ready, n)
                    for kb in range(n % TB + 1):
                        last = turn(ps[:, 4 + kb // 4, (kb % 4) * P:(kb % 4 + 1) * P], psel[:, n % 2, kb * P:(kb + 1) * P])
                    last.then_inc(pT_done, 1)
                for item in lanes[2:]:
                    if item:
                        lane(item)
                if t in M0_SLOTS:
                    if t == M0_SLOTS[0]:
                        pe.wait_ge(stack_in[0], STACK_DMAS)
                    for n in m0_units(t):
                        max_unit(0, 0, n, first=True)
                        if n == MUN_A + 4:
                            row_copy(0, 0)
            pe.wait_ge(spT_ready, 12)
            run(0, STACK_DMAS, 0, first=True)
            with pe.Fori(0, 2) as i:
                run(3 * i + 1, STACK_DMAS * (i + 1), 1)
                run(3 * i + 2, STACK_DMAS * (i + 2), 2)
                run(3 * i + 3, STACK_DMAS * (i + 2), 0)
            run(7, None, 1, last=True)
            for s in range(STEPS - LAG, STEPS):
                values(7, 1, s)
            pe.wait_ge(turned, 2 * NG - 1)
            back(7, 1)

            pe.wait_ge(turned, 2 * NG)
            for c in range(4):
                if c >= 2:
                    pe.wait_ge(aoT_ready, c - 1)
                for i in range(4):
                    t = 4 * c + i
                    b, qi = t // TB, t % TB
                    last = turn(ps[:, c % 2, i * P:(i + 1) * P], ao[:, qi, b * D:(b + 1) * D])
                last.then_inc(aoT_done, 1)
            for t in range(NT):
                pe.wait_ge(aoT_ready, t // 4 + 1)
                if t >= 2:
                    pe.wait_ge(x2_ready, t - 1)
                mm(ps[:, 2 + t % 2, 0:ZW], tT[:, t * P:(t + 1) * P], W("wo", ZM, D), start=True, stop=True).then_inc(proj_done, 1)
            for c in range(4):
                if c >= 2:
                    pe.wait_ge(xfT_ready, c - 1)
                for i in range(4):
                    t = 4 * c + i
                    pe.wait_ge(xf_ready, t + 1)
                    last = turn(ps[:, c % 2, i * P:(i + 1) * P], tmp[:, t, :])
                last.then_inc(xfT_done, 1)
            for t in range(NT):
                pe.wait_ge(xfT_ready, t // 4 + 1)
                last = mm(ps[:, 6, t * E:(t + 1) * E], tT[:, t * P:(t + 1) * P], W("gate"), start=True, stop=True)
            last.then_inc(gate_done, 1)
            for c in range(4):
                r = tT[:, c * CH:(c + 1) * CH]
                for i, (name, wn, nr, hb, src) in enumerate(MOE):
                    n = c * NB + i
                    if n >= 6:
                        pe.wait_ge(hb_read, n - 5)
                        pi = (n - 6) % NB
                        if MOE[pi][0] == "z1":
                            pe.wait_ge(glu_ready, 4 * ((n - 6) // NB) + MOE[pi][3] + 1)
                    if src:
                        pe.wait_ge(hb_read, c * NB + ORDER[(src, nr - 1)] + 1)
                    for q in range(nr):
                        if nr == 1:
                            wt, rr = W(wn, hb * P, (hb + 1) * P), (hid[:, SLOT[(src, 0)], :] if src else r)
                        else:
                            wt, rr = V(wn, q, hb * P, (hb + 1) * P), hid[:, SLOT[(src, q)], :]
                        ins = mm(ps[:, n % 6, :], wt, rr, start=(q == 0), stop=(q == nr - 1))
                    ins.then_inc(hb_done, 1)
                pe.wait_ge(glu_ready, 4 * (c + 1))
                pe.wait_ge(hb_read, NB * (c + 1))
                for t in range(4 * c, 4 * c + 4):
                    if t < 2:
                        pe.wait_ge(gmax_ready, 1)
                    else:
                        pe.wait_ge(out_ready, t - 1)
                    cc = (t % 4) * P
                    for e, (hn, wn) in enumerate((("h0", "e0_down"), ("z1", "e1_down"), ("a3", "e2_l4"), ("u3", "e3_out"))):
                        for q in range(2):
                            ins = mm(ps[:, 6 + t % 2, e * ZW:(e + 1) * ZW], hid[:, SLOT[(hn, q)], cc:cc + P], V(wn, q, ZM, D),
                                     start=(q == 0), stop=(q == 1))
                    ins.then_inc(down_done, 1)


_A = ("Wq", "Wk", "Wv", "Wo")


def kernel(**inputs):
    import numpy as np
    import concourse.bacc as bacc
    from concourse.bass_utils import run_bass_kernel_spmd

    def a(n):
        return np.asarray(inputs["L0_attn_" + n])

    def f(n):
        return np.asarray(inputs["L0_ffn_" + n])

    arrays = {
        "x": np.ascontiguousarray(a("summaries")),
        "wts": np.ascontiguousarray(np.concatenate(
            [a(n) for n in _A] + [f(n).T for n in ("wq", "wk", "wv", "wo", "gate_w", "e0_up", "e1_w1", "e1_w2", "e2_l1", "e3_down", "e3_up")], axis=1)),
        "wts2": np.ascontiguousarray(np.concatenate(
            [f(n).T for n in ("e0_down", "e1_down", "e2_l2", "e2_l3", "e2_l4", "e3_out")], axis=1)),
        "cols": np.ascontiguousarray(np.stack([a("bq"), a("bk"), f("n1_w"), f("n2_w")], axis=1)),
        "rows": np.ascontiguousarray(np.concatenate([a("bv"), a("bo"), f("qn_w"), f("kn_w")])[None]),
    }
    nc = bacc.Bacc("TRN2", target_bir_lowering=False, num_devices=1)
    args = [nc.dram_tensor("in_" + n, v.shape, mybir.dt.from_np(v.dtype), kind="ExternalInput").ap() for n, v in arrays.items()]
    args.append(nc.dram_tensor("out", (B, T, D), F32, kind="ExternalOutput").ap())
    build(nc, *args)
    r = run_bass_kernel_spmd(nc, [{"in_" + n: v for n, v in arrays.items()}], core_ids=[0])
    return r.results[0]["out"]
```

```python
from contextlib import ExitStack

import concourse.bass as bass
from concourse import mybir

F32 = mybir.dt.float32
BF16 = mybir.dt.bfloat16
U32 = mybir.dt.uint32
I32 = mybir.dt.int32
ALU = mybir.AluOpType
ACT = mybir.ActivationFunctionType
AX_X = mybir.AxisListType.X

P = 128
B, T, D = 2, 1024, 128
NT = B * T // P
TB = T // P
TOPK = 8
H, HD = 16, 8
HG = 4
NG = B * H // HG
CH = 512
HID = 256
E = 4
ZM = 32
ZW = D - ZM
NEG = -1.0e30
MARK = -3.0e38
FMAX = 3.4028234663852886e38
LN_EPS = 1e-5
RMS_EPS = 1.1920929e-07
ROWS = 48
PADR = 96
MROW = 96
EROWS = MROW + 3
Q_PARTS = (0, 0, 0, 1, 1, 2)
K_PARTS = (0, 1, 2, 0, 1, 0)
NBUF = 3
STACK_DMAS = 16 * 12
LAG = 2
STEPS = 12
EUNITS = 2 * STEPS
DIAGS = 16

W_COLS = {}
_at = 0
for _name, _n in (("Wq", D), ("Wk", D), ("Wv", D), ("Wo", D), ("qkv", 3 * D), ("wo", D), ("gate", E),
                  ("e0_up", HID), ("e1_w1", HID), ("e1_w2", HID), ("e2_l1", HID), ("e3_down", D), ("e3_up", HID)):
    W_COLS[_name] = (_at, _n)
    _at += _n
W_ALL = _at
W_ATT = 4 * D
V_COLS = {}
_at = 0
for _name, _n in (("e0_down", D), ("e1_down", D), ("e2_l2", HID), ("e2_l3", HID), ("e2_l4", D), ("e3_out", D)):
    V_COLS[_name] = (_at, _n)
    _at += _n
V_ALL = _at


def key_block_steps():
    out = []
    for c in range(2):
        for kb in range(4 * c + 4):
            diag = kb >= 4 * c
            out.append((c, kb, (kb - 4 * c) * P if diag else 0, diag))
    return out


def max_units():
    out = []
    for qi in range(TB):
        if qi >= 4:
            out += [(qi, j, 1, 0, CH, False) for j in range(HG)]
        w = P * (qi % 4 + 1)
        n = max(1, min(HG, CH // w)) if w != 3 * P else 1
        out += [(qi, j, n, CH * (qi // 4), w, True) for j in range(0, HG, n)]
    return out


KSTEPS = key_block_steps()
MUNITS = max_units()
MUN = len(MUNITS)
MUN_A = sum(u[0] < 4 for u in MUNITS)


def units_of_step(s):
    cols = [CH - k[2] for k in KSTEPS]
    return range(MUN * sum(cols[:s]) // sum(cols), MUN * sum(cols[:s + 1]) // sum(cols))


def order_of_step(s, more):
    out = [("e", 0), ("e", 1), ("v", None)]
    units = [("m", n) for n in units_of_step(s)] if more else []
    at = [0, 1, 2, 3]
    for i, m in reversed(list(enumerate(units))):
        out.insert(at[i * 4 // len(units)], m)
    return out


STEP_A = next(s for s in range(STEPS) if units_of_step(s).stop >= MUN_A)
MROWS_STEP = STEP_A + 2
BACK0_STEP = 7
BACK1_STEP = 2


TURNS = []
for _s in range(STEPS):
    TURNS += [(_w, _n) for _w, _n in order_of_step(_s, True) if _w == "m"]
    if _s == 1:
        TURNS.append(("row", 1))
    if _s == BACK1_STEP:
        TURNS.append(("back", 1))
    if _s == MROWS_STEP:
        TURNS.append(("row", 0))
    if _s == BACK0_STEP:
        TURNS.append(("back", 0))
TURN_BANKS = (4, 5, 7)
FIRST_BANKS = (4, 5, 6)
assert len(TURNS) % len(TURN_BANKS) == 0


def turn_bank(what, n, last=False):
    return 7 if last else TURN_BANKS[TURNS.index((what, n)) % len(TURN_BANKS)]


LANE = {w: [] for w in range(40)}
for _w, _items in {
    0: [("xT", 2), ("q", 2)], 1: [("k", 2), ("v", 2)], 2: [("xT", 3), ("q", 3)], 3: [("k", 3), ("v", 3)],
    12: [("hT", 0), ("hT", 1), ("qkv", 0), ("qkv", 1)], 13: [("qkv", 2), ("qkv", 3), ("qkv", 4), ("qkv", 5)],
    14: [("qkv", 6), ("qkv", 7)],
    17: [None, None, ("sp", 0)], 18: [None, None, ("sp", 1), ("sp", 2), ("sp", 3)], 19: [None, None, ("sp", 4), ("sp", 5)],
    20: [("hT", 2), ("hT", 3), ("qkv", 8), ("qkv", 9), ("qkv", 10), ("qkv", 11)],
    21: [("qkv", 12), ("qkv", 13), ("qkv", 14), ("qkv", 15)],
    25: [("sp", 6)], 26: [("sp", 7), ("sp", 8), ("sp", 9), ("sp", 10), ("sp", 11)],
}.items():
    LANE[_w] = _items
NORM_SLOT = (11, 19)
SCALE_SLOT = (12, 20)
SQUARES_SLOT = (14, 14, 20, 21)
RSQRT_SLOT = (14, 21)
SCALE_QK_SLOT = 16
HI_SLOT = (16, 16, 24, 24)
Y_SLOT = (21, 26)
FRONT = 27
M0_SLOTS = range(20, 27)


def lane_bank(item):
    kind, n = item
    if kind in ("hT", "qkv", "sp") and n >= {"hT": 2, "qkv": 8, "sp": 3}[kind]:
        return {"hT": n % 2, "qkv": 2 + n % 2, "sp": n % 2}[kind]
    return 7


def lane_before():
    last, out = {7: ("v", 1)}, {}
    for w in sorted(LANE):
        for item in filter(None, LANE[w]):
            b = lane_bank(item)
            out[item] = last.get(b)
            last[b] = item
    return out


LANE_BEFORE = lane_before()


TAIL = ({0: [("aoT", 0)], 1: [("aoT", 1)], 2: [("proj", 0), ("proj", 1)], 3: [("proj", 2), ("proj", 3)],
         4: [("proj", 4), ("proj", 5)], 5: [("proj", 6), ("proj", 7)], 9: [("xfT", 0)], 10: [("xfT", 1)], 11: [("gate", 0)]},
        {4: [("aoT", 2)], 5: [("aoT", 3)], 6: [("proj", 8)], 7: [("proj", 9)], 8: [("proj", 10)], 9: [("proj", 11)],
         10: [("proj", 12)], 11: [("proj", 13)], 12: [("proj", 14)], 13: [("proj", 15)],
         22: [("xfT", 2)], 24: [("xfT", 3)], 26: [("gate", 1)]})
X2_STEP = 6
X2_BLOCK = 16
BACK_BLOCK = 2
EB = 5


def tail_bank(item):
    kind, n = item
    first = n < {"aoT": 2, "proj": TB, "xfT": 2, "gate": 1}[kind]
    return 4 + n % 2 if first and kind != "gate" else 5


def tail_before():
    last, out = {}, {}
    for part in TAIL:
        for k in sorted(part):
            for item in part[k]:
                out[item] = last.get(tail_bank(item))
                last[tail_bank(item)] = item
    return out


TAIL_BEFORE = tail_before()


def m0_units(w):
    k, n = w - M0_SLOTS.start, len(M0_SLOTS)
    return range(MUN * k // n, MUN * (k + 1) // n)


def build(nc, x, wts, wts2, cols, rows, out):
    ctx = ExitStack()
    with ctx:
        def sb(name, shape, dt=F32):
            return ctx.enter_context(nc.sbuf_tensor(name, shape, dt))

        def sem(name):
            return ctx.enter_context(nc.semaphore(name))

        ps = ctx.enter_context(nc.psum_tensor("ps", [P, 8, CH], F32))
        ident = sb("ident", [P, P])
        identb = sb("identb", [P, P], BF16)
        maskb = sb("maskb", [P, P], BF16)
        w = sb("w", [P, W_ALL])
        w2 = sb("w2", [P, 2, V_ALL])
        col = sb("col", [P, 4])
        warm = sb("warm", [P, 4])
        row = sb("row", [P, 2 * D + 2 * HD])
        xs = sb("xs", [P, NT, D])
        ys = sb("ys", [P, NT, D])
        tmp = sb("tmp", [P, NT, D])
        tT = sb("tT", [P, NT * P])
        st = sb("st", [P, NT, 6])
        mv = sb("mv", [P, NT, 2])
        sm = sb("sm", [P, 8, NT])
        STK = 4096
        AR = STK * NBUF + 6144
        ar = sb("ar", [P, AR])
        qT = ar[:, STK:STK + 2048]
        kT = ar[:, STK + 2048:STK + 4096]
        vv = ar[:, 2 * STK:2 * STK + 2048].rearrange("p (t d) -> p t d", t=NT)
        pselT, prob, repl, psel = (ar[:, 2 * STK + 2048 * i:2 * STK + 2048 * (i + 1)].rearrange("p (n k) -> p n k", n=2) for i in range(1, 5))
        qst = [ar[:, STK * u:STK * u + 2048].bitcast(BF16).rearrange("p (c j t) -> p c j t", c=2, j=HG) for u in range(NBUF)]
        kst = [ar[:, STK * u + 2048:STK * u + 4096].bitcast(BF16).rearrange("p (j t) -> p j t", j=HG) for u in range(NBUF)]
        pt = ar[:, STK * NBUF:AR].rearrange("p (n j t) -> p n j t", n=3, j=HG)
        hid = ar[:, 0:15 * CH].rearrange("p (n t) -> p n t", n=15)
        qk = sb("qk", [P, 2, 4, 2 * D])
        sq = tmp[:].rearrange("p (n two) d -> p n (two d)", two=2)
        hs = sb("hs", [P, 3, TB * 2 * H])
        nqk = sb("nqk", [P, HD])
        parts = sb("parts", [P, 2, 3, 4, 2 * D], BF16)
        partT = sb("partT", [P, 3, 2, CH], BF16)
        va = sb("va", [P, NG, TB, HG * HD])
        vg = [sb(f"vg{u}", [P, TB, HG, 32]) for u in range(NBUF)]
        ao = sb("ao", [P, TB, B * D])
        avs = sb("avs", [P, 2, CH])
        rec = sb("rec", [P, 2, 4, HG])
        mxa = sb("mxa", [P, 3, HG, 4])
        mxm = sb("mxm", [P, 2, HG * 4])
        mxp = sb("mxp", [P, 2, 8, HG * 4], BF16)
        mxT = sb("mxT", [P, 2, P], BF16)
        m8 = sb("m8", [P, NT, 8])
        negm = sb("negm", [P, NT])
        den = sb("den", [P, NT])
        rden = sb("rden", [P, NT])
        aT = sb("aT", [P, 2, P])
        gl = sb("gl", [P, 6, NT, E])
        ga = sb("ga", [P, 3, NT])

        split = nc.dram_tensor("split", [6, B * D, T], BF16, kind="Internal").ap()

        def W(name, a=0, b=None):
            o, n = W_COLS[name]
            return w[:, o + a:o + (n if b is None else b)]

        def V(name, r, a=0, b=None):
            o, n = V_COLS[name]
            return w2[:, r, o + a:o + (n if b is None else b)]

        x_in = [sem(f"x_in{b}") for b in range(B)]
        wa_in = sem("wa_in")
        wf_in = sem("wf_in")
        vec_in = sem("vec_in")
        const_ready = sem("const_ready")
        y_scale_ready = sem("y_scale_ready")
        y_ready = sem("y_ready")
        xn_ready = sem("xn_ready")
        bias_added = sem("bias_added")
        tr_done = sem("tr_done")
        tT_ready = sem("tT_ready")
        q_done = sem("q_done")
        k_done = sem("k_done")
        v_done = sem("v_done")
        q_ready = sem("q_ready")
        k_ready = sem("k_ready")
        v_ready = sem("v_ready")
        scored = sem("scored")
        chosen = sem("chosen")
        exped = sem("exped")
        psel_ready = sem("psel_ready")
        pT_done = sem("pT_done")
        pT_ready = sem("pT_ready")
        av_a = sem("av_a")
        aT_ready = sem("aT_ready")
        wo_done = sem("wo_done")
        x1_ready = sem("x1_ready")
        x1_stats = sem("x1_stats")
        vstep = sem("vstep")
        hT_done = sem("hT_done")
        hT_ready = sem("hT_ready")
        qkv_done = sem("qkv_done")
        qkv_read = sem("qkv_read")
        nqk_ready = sem("nqk_ready")
        ms_ready = sem("ms_ready")
        start_ready = sem("start_ready")
        newton_step = sem("newton_step")
        rsqrt_ready = sem("rsqrt_ready")
        qk_scaled = sem("qk_scaled")
        qk_normed = sem("qk_normed")
        hi_ready = sem("hi_ready")
        r1_ready = sem("r1_ready")
        mid_ready = sem("mid_ready")
        lo_ready = sem("lo_ready")
        spT_done = sem("spT_done")
        spT_ready = sem("spT_ready")
        spT_stored = [sem(f"spT_stored{p}") for p in range(3)]
        pad_zero = sem("pad_zero")
        pads_ready = sem("pads_ready")
        stack_in = [sem(f"stack_in{u}") for u in range(NBUF)]
        m_scored = sem("m_scored")
        m_reduced = sem("m_reduced")
        max_step = sem("max_step")
        m_parts = sem("m_parts")
        m_rows_done = sem("m_rows_done")
        m_rows_ready = sem("m_rows_ready")
        rows_in = [sem(f"rows_in{h}") for h in range(2)]
        turned = sem("turned")
        e_scored = sem("e_scored")
        e_exped = sem("e_exped")
        unit_taken = sem("unit_taken")
        diag_done = sem("diag_done")
        vg_ready = sem("vg_ready")
        av_done = sem("av_done")
        avs_ready = sem("avs_ready")
        back_done = sem("back_done")
        norm_step = sem("norm_step")
        aoT_done = sem("aoT_done")
        aoT_ready = sem("aoT_ready")
        proj_done = sem("proj_done")
        x2_ready = sem("x2_ready")
        xf_ready = sem("xf_ready")
        xfT_done = sem("xfT_done")
        xfT_ready = sem("xfT_ready")
        gate_done = sem("gate_done")
        gate_exp = sem("gate_exp")
        gmax_ready = sem("gmax_ready")
        hb_done = sem("hb_done")
        hb_read = sem("hb_read")
        glu_ready = sem("glu_ready")
        down_done = sem("down_done")
        out_ready = sem("out_ready")
        out_sent = sem("out_sent")

        block = ctx.enter_context(nc.Block())

        MOE = []
        for hb in range(2):
            MOE.append(("h0", "e0_up", 1, hb, None))
        for hb in range(2):
            MOE.append(("a1", "e2_l1", 1, hb, None))
        for hb in range(2):
            MOE.append(("z1", "e1_w1", 1, hb, None))
        MOE.append(("d3", "e3_down", 1, 0, None))
        for hb in range(2):
            MOE.append(("a2", "e2_l2", 2, hb, "a1"))
        for hb in range(2):
            MOE.append(("z2", "e1_w2", 1, hb, None))
        for hb in range(2):
            MOE.append(("u3", "e3_up", 1, hb, "d3"))
        for hb in range(2):
            MOE.append(("a3", "e2_l3", 2, hb, "a2"))
        NB = len(MOE)
        SLOT = {}
        for name, _, _, hb, _ in MOE:
            SLOT[(name, hb)] = len(SLOT)
        ORDER = {(m[0], m[3]): i for i, m in enumerate(MOE)}

        def norm_x1_rsqrt(b):
            bt = slice(b * TB, (b + 1) * TB)
            return sm[:, 4:6, bt], sm[:, 0:2, bt], sm[:, 6:8, bt]

        def heads_rsqrt():
            return hs[:, 1, :], hs[:, 0, :], hs[:, 2, :]

        def heads_of(z):
            return qk[:, z % 2].rearrange("p t (h d) -> p (t h) d", d=HD)

        def head_scales(z):
            return hs[:, 1, (z % 2) * 8 * H:(z % 2 + 1) * 8 * H].unsqueeze(2).to_broadcast([P, 8 * H, HD])

        @block.sync
        def _(sp):
            xt = x.rearrange("b (t p) d -> p (b t) d", p=P)
            for b in range(B):
                sp.dma_start(xs[:, b * TB:(b + 1) * TB, :], xt[:, b * TB:(b + 1) * TB, :]).then_inc(x_in[b], 16)

            def load_part(g, u, part):
                src = split[:, bass.ds(g * 32, 32), :]
                for p in range(6):
                    if Q_PARTS[p] == part:
                        one = src[part].rearrange("(j d) (c t) -> d c j t", d=HD, c=2)
                        sp.dma_start(qst[u][8 * p:8 * p + 8], one).then_inc(stack_in[u], 16)
                    if K_PARTS[p] == part:
                        one = src[3 + part].rearrange("(j d) t -> d j t", d=HD)
                        sp.dma_start(kst[u][8 * p:8 * p + 8], one).then_inc(stack_in[u], 16)

            def load_stacks(g, u):
                for part in range(3):
                    load_part(g, u, part)

            def load_rows(g, u, h):
                sp.wait_ge(m_rows_ready, 2 * g + h + 1)
                sp.dma_start(qst[u][MROW:MROW + 3, h].rearrange("p j (i t) -> p (j i) t", i=4),
                             mxT[0:48, h, :]).then_inc(rows_in[h], 16)

            def run(g, u, more, first=False, last=False):
                if more:
                    if not first:
                        sp.wait_ge(e_scored, g * EUNITS)
                    load_stacks(g + 2, (u + 2) % NBUF)
                load_rows(g, u, 1)
                if not last:
                    load_rows(g + 1, (u + 1) % NBUF, 0)

            sp.wait_ge(pads_ready, 1)
            for part in range(3):
                sp.wait_ge(spT_stored[part], 16 * 2)
                load_part(0, 0, part)
            sp.wait_ge(pads_ready, 2)
            load_stacks(1, 1)
            load_rows(0, 0, 0)
            sp.wait_ge(pads_ready, NBUF)
            for g in range(NG):
                if g == 2:
                    for p in range(3):
                        sp.wait_ge(spT_stored[p], 16 * 4)
                run(g, g % NBUF, g < NG - 2, first=(g == 0), last=(g == NG - 1))
            ot = out.rearrange("b (t p) d -> p (b t) d", p=P)
            for c in range(4):
                sp.wait_ge(out_ready, 4 * (c + 1))
                sp.dma_start(ot[:, 4 * c:4 * c + 4, :], xs[:, 4 * c:4 * c + 4, :]).then_inc(out_sent, 16)
            sp.wait_ge(out_sent, 64)

        @block.gpsimd
        def _(pool):
            pool.memset(ident[:], 0.0).then_inc(const_ready, 1)
            pool.memset(identb[:], 0.0).then_inc(const_ready, 1)
            pool.memset(maskb[:], 0.0).then_inc(const_ready, 1)
            pool.wait_ge(const_ready, 3)
            for m in (ident, identb):
                pool.affine_select(out=m[:], in_=m[:], compare_op=ALU.not_equal, fill=1.0, base=0,
                                   pattern=[[-1, P]], channel_multiplier=1).then_inc(const_ready, 1)
            pool.affine_select(out=maskb[:], in_=maskb[:], compare_op=ALU.is_ge, fill=NEG, base=0,
                               pattern=[[-1, P]], channel_multiplier=1).then_inc(const_ready, 1)
            for u in range(NBUF):
                pool.memset(vg[u][:], 0.0).then_inc(const_ready, 1)
            pool.memset(mxp[:], 0.0)
            pool.wait_ge(const_ready, 9)
            for u in range(NBUF):
                pool.memset(vg[u][:, :, :, HD:HD + 1], 1.0).then_inc(const_ready, 1)

            def zero_pads(u):
                if u == 1:
                    pool.wait_ge(x1_ready, NT)
                pool.memset(ar[:, STK * u:STK * (u + 1)], 0.0).then_inc(pad_zero, 1)
                pool.wait_ge(pad_zero, u + 1)
                pool.memset(kst[u][MROW:MROW + 3], 1.0).then_inc(pads_ready, 1)
                pool.wait_ge(pads_ready, u + 1)

            newton = [0]

            def step(ins):
                newton[0] += 1
                ins.then_inc(newton_step, 1)
                pool.wait_ge(newton_step, newton[0])

            def rsqrt_steps(n, y, val, scratch):
                pool.wait_ge(start_ready, n)
                for i in range(3):
                    step(pool.tensor_tensor(scratch, y, y, ALU.mult))
                    step(pool.tensor_tensor(scratch, scratch, val, ALU.mult))
                    step(pool.tensor_scalar(scratch, scratch, -0.5, 1.5, ALU.mult, ALU.add))
                    last = pool.tensor_tensor(y, y, scratch, ALU.mult)
                    if i < 2:
                        step(last)
                last.then_inc(rsqrt_ready, 1)

            zero_pads(0)
            pool.wait_ge(vec_in, 32)
            pool.wait_ge(xn_ready, NT)
            pool.tensor_tensor(xs[:], xs[:], row[:, D:2 * D].unsqueeze(1).to_broadcast([P, NT, D]), ALU.add).then_inc(bias_added, 1)
            pool.tensor_tensor(nqk[:], row[:, 2 * D:2 * D + HD], row[:, 2 * D + HD:2 * D + 2 * HD], ALU.mult).then_inc(nqk_ready, 1)
            pool.wait_ge(nqk_ready, 1)
            for z in range(4):
                if z % 2 == 0:
                    rsqrt_steps(z + 1, *norm_x1_rsqrt(z // 2))
                    if z:
                        zero_pads(1)
                    rsqrt_steps(z + 2, *heads_rsqrt())
                if z >= 2:
                    if z == 2:
                        pool.wait_ge(rsqrt_ready, 4)
                    pool.tensor_tensor(heads_of(z), heads_of(z), head_scales(z), ALU.mult).then_inc(qk_scaled, 1)
                pool.wait_ge(qk_scaled, z + 1)
                k4 = qk[:, z % 2, :, D:2 * D].rearrange("p t (h d) -> p t h d", h=H)
                pool.tensor_tensor(k4, k4, nqk[:].unsqueeze(1).unsqueeze(1).to_broadcast([P, 4, H, HD]), ALU.mult).then_inc(qk_normed, 1)

            def copy_v(g, u):
                pool.tensor_copy(vg[u][:, :, :, 0:HD],
                                 va[:, bass.ds(g, 1)].rearrange("p o k (j d) -> p (o k) j d", j=HG)).then_inc(vg_ready, 1)

            pool.wait_ge(qkv_read, NT)
            copy_v(0, 0)
            zero_pads(2)

            def run(g, u, first=False, last=False):
                for s, (c, kb, off, diag) in enumerate(KSTEPS):
                    if diag:
                        for jj in range(2):
                            pool.wait_ge(e_exped, g * EUNITS + 2 * s + jj + 1)
                            pool.sem_inc(unit_taken, 1)
                            v = pt[:, s % 3, 2 * jj:2 * jj + 2, off:off + P]
                            pool.affine_select(out=v, in_=v, compare_op=ALU.is_ge, fill=0.0, base=0,
                                               pattern=[[0, 2], [1, P]], channel_multiplier=-1).then_inc(diag_done, 1)
                    if s == 4 and not last:
                        if not first:
                            pool.wait_ge(av_done, (g - 1) * STEPS + 1)
                        copy_v(g + 1, (u + 1) % NBUF)

            run(0, 0, first=True)
            with pool.Fori(0, 2) as i:
                run(3 * i + 1, 1)
                run(3 * i + 2, 2)
                run(3 * i + 3, 0)
            run(7, 1, last=True)

        @block.scalar
        def _(act):
            act.dma_start(w[:, 0:W_ATT], wts[:, 0:W_ATT]).then_inc(wa_in, 16)
            act.dma_start(col[:], cols).then_inc(vec_in, 16)
            act.dma_start(row[:], rows.to_broadcast([P, 2 * D + 2 * HD])).then_inc(vec_in, 16)
            act.dma_start(w[:, W_ATT:W_ALL], wts[:, W_ATT:W_ALL]).then_inc(wf_in, 16)
            act.dma_start(w2[:], wts2.rearrange("(r p) n -> p r n", p=P)).then_inc(wf_in, 16)
            act.wait_ge(vec_in, 32)
            nc.scalar.activation(warm[:], col[:], ACT.Exp)

            def lane(item):
                kind, n = item
                bank = ps[:, lane_bank(item), :]
                cols_ = slice(n * CH, (n + 1) * CH)
                if kind == "xT":
                    act.wait_ge(tr_done, n + 1)
                    nc.scalar.copy(tT[:, cols_], bank).then_inc(tT_ready, 1)
                elif kind == "q":
                    act.wait_ge(q_done, n + 1)
                    nc.scalar.activation(qT[:, cols_], bank, ACT.Identity, bias=col[:, 0:1]).then_inc(q_ready, 1)
                elif kind == "hT":
                    act.wait_ge(hT_done, n + 1)
                    nc.scalar.activation(tT[:, cols_], bank, ACT.Copy, scale=col[:, 2:3]).then_inc(hT_ready, 1)
                elif kind == "qkv":
                    z = n // 4
                    act.wait_ge(qkv_done, n + 1)
                    if n % 4 == 0 and z >= 2:
                        act.wait_ge(lo_ready, z - 1)
                    if n % TB == 0:
                        act.wait_ge(hT_done, 2 * (n // TB) + 2)
                    nc.scalar.copy(qk[:, z % 2, n % 4, :], bank[:, 0:2 * D])
                    nc.scalar.activation(sq[:, n % TB, :], bank[:, 0:2 * D], ACT.Square)
                    nc.scalar.copy(va[:, 4 * (n // TB):4 * (n // TB) + 4, n % TB, :],
                                   bank[:, 2 * D:3 * D].rearrange("p (g d) -> p g d", g=4)).then_inc(qkv_read, 1)
                elif kind == "sp":
                    z, p = n // 3, n % 3
                    act.wait_ge(spT_done, n + 1)
                    if z:
                        act.wait_ge(spT_stored[p], 16 * z)
                    nc.scalar.copy(partT[:, p].rearrange("p s t -> p (s t)"), bank.bitcast(BF16)).then_inc(spT_ready, 1)
                    act.wait_ge(spT_ready, n + 1)
                    b, q = z // 2, z % 2
                    act.dma_start(split.rearrange("(s q) f t -> q f s t", s=2)[p][b * D:(b + 1) * D, :, q * CH:(q + 1) * CH],
                                  partT[:, p]).then_inc(spT_stored[p], 16)

            def row_copy(g, h, first=False, last=False):
                act.wait_ge(m_rows_done, 2 * g + h + 1)
                if not first:
                    act.wait_ge(rows_in[h], 16 * g)
                bank = 7 if first and h == 0 else turn_bank("row", h, last)
                nc.scalar.copy(mxT[0:48, h, :], ps[0:48, bank, 0:64].bitcast(BF16)).then_inc(m_rows_ready, 1)

            for c in range(2):
                act.wait_ge(tr_done, c + 1)
                nc.scalar.copy(tT[:, c * CH:(c + 1) * CH], ps[:, c, :]).then_inc(tT_ready, 1)
            for c in range(2):
                act.wait_ge(q_done, c + 1)
                nc.scalar.activation(qT[:, c * CH:(c + 1) * CH], ps[:, 2 + c, :], ACT.Identity,
                                     bias=col[:, 0:1]).then_inc(q_ready, 1)
            for t in range(FRONT):
                lanes = LANE[t] + [None] * 3
                if lanes[0]:
                    lane(lanes[0])
                if 3 <= t < NT + 3:
                    n = t - 3
                    act.wait_ge(av_a, n + 1)
                    if n >= 2:
                        act.wait_ge(wo_done, n - 1)
                    nc.scalar.copy(aT[:, n % 2, :], ps[:, 6, 0:P]).then_inc(aT_ready, 1)
                if lanes[1]:
                    lane(lanes[1])
                if t < NT:
                    wdt = P * (t % TB + 1)
                    act.wait_ge(chosen, t + 1)
                    if t >= 2:
                        act.wait_ge(psel_ready, t - 1)
                    nc.scalar.activation(prob[:, t % 2, 0:wdt], ps[:, 2 * (t % 2):2 * (t % 2) + 2, :].rearrange("p a b -> p (a b)")[:, 0:wdt],
                                         ACT.Exp, bias=negm[:, t:t + 1], scale=float(D) ** -0.5).then_inc(exped, 1)
                if 2 <= t < NT + 2:
                    n = t - 2
                    wdt = P * (n % TB + 1)
                    act.wait_ge(pT_done, n + 1)
                    if n >= 2:
                        act.wait_ge(av_a, n - 1)
                    nc.scalar.copy(pselT[:, n % 2, 0:wdt], ps[:, 4:6, :].rearrange("p a b -> p (a b)")[:, 0:wdt]).then_inc(pT_ready, 1)
                for z in range(4):
                    if t == HI_SLOT[z]:
                        act.wait_ge(qk_normed, z + 1)
                        if z >= 2:
                            act.wait_ge(spT_done, 3 * (z - 1))
                        nc.scalar.copy(parts[:, z % 2, 0], qk[:, z % 2]).then_inc(hi_ready, 1)
                    if t == HI_SLOT[z] + 1:
                        act.wait_ge(r1_ready, z + 1)
                        nc.scalar.copy(parts[:, z % 2, 1], qk[:, z % 2]).then_inc(mid_ready, 1)
                for item in lanes[2:]:
                    if item:
                        lane(item)
                if t in M0_SLOTS and MUN_A + 4 in m0_units(t):
                    row_copy(0, 0, first=True)
                if t in Y_SLOT:
                    b = Y_SLOT.index(t)
                    act.wait_ge(y_scale_ready, b + 1)
                    for n in range(b * TB, (b + 1) * TB):
                        nc.scalar.activation(ys[:, n, :], xs[:, n, :], ACT.Identity, bias=sm[:, 3, n:n + 1],
                                             scale=sm[:, 4, n:n + 1]).then_inc(y_ready, 1)

            def run(g, first=False, last=False):
                for s, (c, kb, off, diag) in enumerate(KSTEPS):
                    for jj in range(2):
                        act.wait_ge(e_scored, g * EUNITS + 2 * s + jj + 1)
                        if jj == 0 and not (first and s < 3):
                            act.wait_ge(av_done, g * STEPS + s - 2)
                        nc.scalar.activation(pt[:, s % 3, 2 * jj:2 * jj + 2, off:CH], ps[:, 2 * jj:2 * jj + 2, off:CH],
                                             ACT.Exp, scale=float(HD) ** -0.5).then_inc(e_exped, 1)
                    if s == 1:
                        row_copy(g, 1, first, last)
                    if s == MROWS_STEP and not last:
                        row_copy(g + 1, 0)
                    if last:
                        for item in TAIL[0].get(s, ()):
                            if item[0] == "gate":
                                tail(item)

            def tail(item):
                kind, n = item
                bank = ps[:, tail_bank(item), :]
                if kind == "aoT":
                    act.wait_ge(aoT_done, n + 1)
                    nc.scalar.copy(tT[:, n * CH:(n + 1) * CH], bank).then_inc(aoT_ready, 1)
                elif kind == "xfT":
                    act.wait_ge(xfT_done, n + 1)
                    nc.scalar.activation(tT[:, n * CH:(n + 1) * CH], bank, ACT.Copy, scale=col[:, 3:4]).then_inc(xfT_ready, 1)
                elif kind == "gate":
                    act.wait_ge(gmax_ready, n + 1)
                    bt = slice(n * TB, (n + 1) * TB)
                    nc.scalar.activation(gl[:, 2, bt], gl[:, 1, bt], ACT.Exp).then_inc(gate_exp, 1)

            run(0, first=True)
            with act.Fori(0, 2) as i:
                for k in (1, 2, 3):
                    run(3 * i + k)
            run(7, last=True)

            for c in range(4):
                for i, (name, wn, nr, hb, src) in enumerate(MOE):
                    n = c * NB + i
                    for item in TAIL[1].get(n, ()):
                        tail(item)
                    act.wait_ge(hb_done, n + 1)
                    if c and i == 0:
                        act.wait_ge(down_done, 4 * c)
                    o = hid[:, SLOT[(name, hb)], :]
                    bank = ps[:, n % EB, :]
                    if name == "z1":
                        nc.scalar.activation(o, bank, ACT.Tanh, scale=0.5).then_inc(hb_read, 1)
                    elif name == "z2":
                        nc.scalar.copy(o, bank).then_inc(hb_read, 1)
                    else:
                        nc.scalar.activation(o, bank, ACT.Gelu).then_inc(hb_read, 1)

        @block.vector
        def _(dve):
            v = nc.vector
            count = [0]

            def link(ins):
                count[0] += 1
                ins.then_inc(vstep, 1)
                dve.wait_ge(vstep, count[0])

            def rsqrt(y, val, scratch):
                link(v.tensor_scalar(y.bitcast(U32), val.bitcast(U32), 1, None, ALU.logical_shift_right))
                link(v.tensor_scalar(y.bitcast(I32), y.bitcast(I32), -1.0, float(0x5f3759df), ALU.mult, ALU.add))
                for _ in range(3):
                    link(v.tensor_tensor(scratch, y, y, ALU.mult))
                    link(v.scalar_tensor_tensor(out=scratch, in0=scratch, scalar=-0.5, in1=val, op0=ALU.mult, op1=ALU.mult))
                    link(v.scalar_tensor_tensor(out=y, in0=scratch, scalar=1.5, in1=y, op0=ALU.add, op1=ALU.mult))

            def rsqrt_start(y, val, scratch):
                link(v.tensor_scalar(y.bitcast(U32), val.bitcast(U32), 1, None, ALU.logical_shift_right))
                v.tensor_scalar(y.bitcast(I32), y.bitcast(I32), -1.0, float(0x5f3759df), ALU.mult, ALU.add).then_inc(start_ready, 1)

            def stats(src, tiles):
                for t in tiles:
                    last = v.bn_stats(st[:, t, :], src[:, t, :])
                link(last)
                for t in tiles:
                    last = v.bn_aggr(mv[:, t, :], st[:, t, :])
                link(last)

            def norm_tiles(tiles):
                for t in tiles:
                    v.tensor_scalar(tmp[:, t, :], xs[:, t, :], mv[:, t, 0:1], sm[:, 4, t:t + 1], ALU.subtract, ALU.mult).then_inc(xn_ready, 1)

            for b in range(B):
                dve.wait_ge(x_in[b], 16)
                tiles = range(b * TB, (b + 1) * TB)
                bt = slice(b * TB, (b + 1) * TB)
                stats(xs, tiles)
                link(v.tensor_scalar(sm[:, 0, bt], mv[:, bt, 1], LN_EPS, None, ALU.add))
                rsqrt(sm[:, 4, bt], sm[:, 0, bt], sm[:, 7, bt])
                if b == 0:
                    norm_tiles(tiles)
            norm_tiles(range(TB, TB + 4))
            dve.wait_ge(vec_in, 32)

            def take_k(c, bank):
                dve.wait_ge(k_done, c + 1)
                v.tensor_scalar(kT[:, c * CH:(c + 1) * CH], ps[:, bank, :], col[:, 1:2], None, ALU.add).then_inc(k_ready, 1)

            def take_v(c, bank):
                dve.wait_ge(v_done, c + 1)
                v.tensor_tensor(vv[:, 4 * c:4 * c + 4, :], ps[:, bank, :].rearrange("p (t d) -> p t d", t=4),
                                row[:, 0:D].unsqueeze(1).to_broadcast([P, 4, D]), ALU.add).then_inc(v_ready, 1)

            for c in range(2):
                take_k(c, 4 + c)
                take_v(c, 6 + c)
            norm_tiles(range(TB + 4, NT))

            def reduce_unit(g, n, first=False):
                qi, j, nh, k0, wdt, diag = MUNITS[n]
                if n == 0 and not first:
                    dve.wait_ge(max_step, 8 * g - 3)
                dve.wait_ge(m_scored, g * MUN + n + 1)
                which = 0 if qi < 4 else (2 if diag else 1)
                v.tensor_reduce(mxa[:, which, j:j + nh, qi % 4], ps[:, FIRST_BANKS[n % 3] if first else turn_bank("m", n), 0:nh * wdt].rearrange("p (j k) -> p j k", j=nh),
                                AX_X, ALU.max).then_inc(m_reduced, 1)

            def split_maxima(g, h, first=False):
                a = mxa[:, 0 if h == 0 else 1].rearrange("p j i -> p (j i)")
                b = mxa[:, 0 if h == 0 else 2].rearrange("p j i -> p (j i)")
                base = (2 * g + h) * 4
                dve.wait_ge(m_reduced, g * MUN + (MUN_A if h == 0 else MUN))
                if not (first and h == 0):
                    dve.wait_ge(m_parts, 2 * g + h)
                v.tensor_tensor(mxm[:, 0], a, b, ALU.max).then_inc(max_step, 1)
                dve.wait_ge(max_step, base + 1)
                if not first:
                    dve.wait_ge(m_rows_done, 2 * g + h - 1)
                v.tensor_scalar(mxp[:, h, 0], mxm[:, 0], -1.0, None, ALU.mult).then_inc(max_step, 1)
                dve.wait_ge(max_step, base + 2)
                v.scalar_tensor_tensor(out=mxm[:, 1], in0=mxm[:, 0], scalar=-1.0, in1=mxp[:, h, 0],
                                       op0=ALU.mult, op1=ALU.subtract).then_inc(max_step, 1)
                dve.wait_ge(max_step, base + 3)
                v.tensor_copy(mxp[:, h, 1], mxm[:, 1]).then_inc(max_step, 1)
                dve.wait_ge(max_step, base + 4)
                v.tensor_tensor(mxp[:, h, 2], mxm[:, 1], mxp[:, h, 1], ALU.subtract).then_inc(m_parts, 1)

            def take_sums(g, c, first=False):
                dve.wait_ge(av_done, g * STEPS + (4 if c == 0 else STEPS))
                if not first:
                    dve.wait_ge(back_done, 2 * g + c)
                v.tensor_copy(avs[:, c, :], ps[:, 6, :]).then_inc(avs_ready, 1)

            def normalise(g, c, first=False, last=False):
                dve.wait_ge(back_done, 2 * g + c + 1)
                t4 = ps[:, turn_bank("back", c, last), :].rearrange("p (i j d) -> p i j d", i=4, j=HG)
                if not first:
                    dve.wait_ge(turned, 2 * g + c)
                v.reciprocal(rec[:, c], t4[:, :, :, HD]).then_inc(norm_step, 1)
                dve.wait_ge(norm_step, 2 * g + c + 1)
                o = ao[:, 4 * c:4 * c + 4, bass.ds(g * HG * HD, HG * HD)].rearrange("p i (j d) -> p i j d", j=HG)
                v.tensor_tensor(o, t4[:, :, :, 0:HD], rec[:, c].unsqueeze(3).to_broadcast([P, 4, HG, HD]), ALU.mult).then_inc(turned, 1)

            def add_projection(t):
                if t == 0:
                    dve.wait_ge(y_ready, NT)
                dve.wait_ge(proj_done, t + 1)
                v.tensor_tensor(ys[:, t, ZM:D], ys[:, t, ZM:D], ps[:, tail_bank(("proj", t)), 0:ZW], ALU.add).then_inc(x2_ready, 1)

            def norm_x2(b):
                tiles = range(b * TB, (b + 1) * TB)
                bt = slice(b * TB, (b + 1) * TB)
                dve.wait_ge(x2_ready, (b + 1) * TB)
                stats(ys, tiles)
                link(v.tensor_tensor(sm[:, 2, bt], mv[:, bt, 0], mv[:, bt, 0], ALU.mult))
                link(v.tensor_tensor(sm[:, 2, bt], sm[:, 2, bt], mv[:, bt, 1], ALU.add))
                link(v.tensor_scalar(sm[:, 0, bt], sm[:, 2, bt], RMS_EPS, None, ALU.add))
                rsqrt(sm[:, 4, bt], sm[:, 0, bt], sm[:, 7, bt])
                for t in tiles:
                    v.tensor_scalar(tmp[:, t, :], ys[:, t, :], sm[:, 4, t:t + 1], None, ALU.mult).then_inc(xf_ready, 1)
                link(v.tensor_tensor(xs[:, bt], xs[:, bt], ys[:, bt], ALU.add))

            def gate_logits(b):
                bt = slice(b * TB, (b + 1) * TB)
                raw, logit, num, prb, win, cmp_ = (gl[:, i, bt] for i in range(6))
                top, total, inv = (ga[:, i, bt] for i in range(3))
                dve.wait_ge(gate_done, b + 1)
                link(v.tensor_copy(raw, ps[:, tail_bank(("gate", b)), 0:TB * E].rearrange("p (t e) -> p t e", t=TB)))
                link(v.tensor_tensor(cmp_, raw, raw, ALU.is_equal))
                link(v.memset(logit, 0.0))
                link(v.copy_predicated(logit, cmp_.bitcast(U32), raw))
                link(v.tensor_scalar(logit, logit, FMAX, -FMAX, ALU.min, ALU.max))
                link(v.tensor_reduce(top, logit, AX_X, ALU.max))
                v.tensor_tensor(logit, logit, top.unsqueeze(2).to_broadcast([P, TB, E]), ALU.subtract).then_inc(gmax_ready, 1)

            def gate_weights(b):
                bt = slice(b * TB, (b + 1) * TB)
                raw, logit, num, prb, win, cmp_ = (gl[:, i, bt] for i in range(6))
                top, total, inv = (ga[:, i, bt] for i in range(3))
                dve.wait_ge(gate_exp, b + 1)
                link(v.tensor_reduce(total, num, AX_X, ALU.add))
                link(v.reciprocal(inv, total))
                link(v.tensor_tensor(prb, num, inv.unsqueeze(2).to_broadcast([P, TB, E]), ALU.mult))
                link(v.memset(win, 0.0))
                for a in range(E):
                    for o in range(a + 1, E):
                        link(v.tensor_tensor(cmp_[:, :, 0], prb[:, :, a], prb[:, :, o], ALU.is_ge))
                        v.tensor_tensor(win[:, :, a], win[:, :, a], cmp_[:, :, 0], ALU.add)
                        link(v.scalar_tensor_tensor(out=win[:, :, o], in0=win[:, :, o], scalar=1.0, in1=cmp_[:, :, 0],
                                                    op0=ALU.add, op1=ALU.subtract))
                link(v.scalar_tensor_tensor(out=prb, in0=win, scalar=2.0, in1=prb, op0=ALU.is_ge, op1=ALU.mult))
                link(v.tensor_reduce(total, prb, AX_X, ALU.add))
                link(v.tensor_scalar(total, total, 1e-8, None, ALU.add))
                link(v.reciprocal(inv, total))
                link(v.tensor_tensor(prb, prb, inv.unsqueeze(2).to_broadcast([P, TB, E]), ALU.mult))

            def run(g, first=False, last=False):
                for s in range(STEPS):
                    if s == 2 and not first:
                        take_sums(g - 1, 1)
                    if s == BACK1_STEP + 1 and not first:
                        normalise(g - 1, 1, last=last)
                    if s == 4 + LAG:
                        take_sums(g, 0, first)
                    if s == BACK0_STEP + 1:
                        normalise(g, 0, first, last)
                    if not last:
                        for n in units_of_step(s):
                            reduce_unit(g + 1, n)
                        if s == STEP_A:
                            split_maxima(g + 1, 0)
                    else:
                        for kind, t in TAIL[0].get(s, ()):
                            bank = ps[:, tail_bank((kind, t)), :]
                            cols_ = slice(t * CH, (t + 1) * CH)
                            if kind == "aoT":
                                dve.wait_ge(aoT_done, t + 1)
                                v.tensor_copy(tT[:, cols_], bank).then_inc(aoT_ready, 1)
                            if kind == "proj":
                                add_projection(t)
                            if kind == "xfT":
                                dve.wait_ge(xfT_done, t + 1)
                                v.tensor_scalar(tT[:, cols_], bank, col[:, 3:4], None, ALU.mult).then_inc(xfT_ready, 1)
                        if s == X2_STEP:
                            norm_x2(0)
                if not last:
                    split_maxima(g + 1, 1)

            def norm_x1(b):
                tiles = range(b * TB, (b + 1) * TB)
                bt = slice(b * TB, (b + 1) * TB)
                dve.wait_ge(x1_stats, (b + 1) * TB)
                for t in tiles:
                    last = v.bn_aggr(mv[:, t, :], st[:, t, :])
                link(last)
                link(v.tensor_scalar(sm[:, 0, bt], mv[:, bt, 1], LN_EPS, None, ALU.add))
                link(v.scalar_tensor_tensor(out=sm[:, 1, bt], in0=sm[:, 0, bt], scalar=RMS_EPS, in1=mv[:, bt, 1],
                                            op0=ALU.mult, op1=ALU.add))
                rsqrt_start(*norm_x1_rsqrt(b))

            def scale_x1(b):
                tiles = range(b * TB, (b + 1) * TB)
                bt = slice(b * TB, (b + 1) * TB)
                dve.wait_ge(rsqrt_ready, 2 * b + 1)
                v.scalar_tensor_tensor(out=sm[:, 3, bt], in0=mv[:, bt, 0], scalar=-1.0, in1=sm[:, 4, bt],
                                       op0=ALU.mult, op1=ALU.mult).then_inc(y_scale_ready, 1)
                for t in tiles:
                    v.tensor_scalar(tmp[:, t, :], xs[:, t, :], mv[:, t, 0:1], sm[:, 5, t:t + 1], ALU.subtract, ALU.mult).then_inc(xn_ready, 1)

            for t in range(FRONT):
                if 4 <= t < NT + 4:
                    n = t - 4
                    dve.wait_ge(psel_ready, n + 1)
                    link(v.reciprocal(rden[:, n:n + 1], den[:, n:n + 1]))
                    dve.wait_ge(wo_done, n + 1)
                    if n == 0:
                        dve.wait_ge(bias_added, 1)
                    v.scalar_tensor_tensor(out=xs[:, n, :], in0=ps[:, 6, 0:D], scalar=rden[:, n:n + 1], in1=xs[:, n, :],
                                           op0=ALU.mult, op1=ALU.add).then_inc(x1_ready, 1)
                for item in filter(None, LANE[t]):
                    if item[0] == "k":
                        take_k(item[1], 7)
                    if item[0] == "v":
                        take_v(item[1], 7)
                if t < NT:
                    wdt = P * (t % TB + 1)
                    dve.wait_ge(scored, t + 1)
                    s = ps[:, 2 * (t % 2):2 * (t % 2) + 2, :].rearrange("p a b -> p (a b)")[:, 0:wdt]
                    link(v.max(m8[:, t, :], s))
                    if t >= 2:
                        dve.wait_ge(psel_ready, t - 1)
                    v.tensor_scalar(negm[:, t:t + 1], m8[:, t, 0:1], -float(D) ** -0.5, None, ALU.mult)
                    v.match_replace(out=repl[:, t % 2, 0:wdt], in_to_replace=m8[:, t, :], in_values=s, imm_value=MARK).then_inc(chosen, 1)
                if t in SCALE_SLOT:
                    scale_x1(SCALE_SLOT.index(t))
                if 4 <= t < NT + 4:
                    dve.wait_ge(x1_ready, n + 1)
                    v.bn_stats(st[:, n, :], xs[:, n, :]).then_inc(x1_stats, 1)
                if 1 <= t < NT + 1:
                    n = t - 1
                    wdt = P * (n % TB + 1)
                    dve.wait_ge(exped, n + 1)
                    if n >= 2:
                        dve.wait_ge(pT_done, n - 1)
                    v.scalar_tensor_tensor(out=psel[:, n % 2, 0:wdt], in0=repl[:, n % 2, 0:wdt], scalar=MARK, in1=prob[:, n % 2, 0:wdt],
                                           op0=ALU.is_equal, op1=ALU.mult, accum_out=den[:, n:n + 1]).then_inc(psel_ready, 1)
                if t in NORM_SLOT:
                    norm_x1(NORM_SLOT.index(t))
                for z in range(4):
                    one = qk[:, z % 2]
                    if t == HI_SLOT[z] + 2:
                        dve.wait_ge(mid_ready, z + 1)
                        v.tensor_tensor(parts[:, z % 2, 2], one, parts[:, z % 2, 1], ALU.subtract).then_inc(lo_ready, 1)
                    if t == HI_SLOT[z] + 1:
                        dve.wait_ge(hi_ready, z + 1)
                        v.tensor_tensor(one, one, parts[:, z % 2, 0], ALU.subtract).then_inc(r1_ready, 1)
                for z in range(4):
                    if t == SQUARES_SLOT[z]:
                        dve.wait_ge(qkv_read, 4 * (z + 1))
                        if z == 2:
                            dve.wait_ge(qk_scaled, 2)
                        half = slice((z % 2) * 8 * H, (z % 2 + 1) * 8 * H)
                        v.tensor_reduce(hs[:, 1, half], sq[:, 4 * (z % 2):4 * (z % 2) + 4, :].rearrange("p t (h d) -> p (t h) d", d=HD),
                                        AX_X, ALU.add).then_inc(ms_ready, 1)
                if t in RSQRT_SLOT:
                    dve.wait_ge(ms_ready, 2 * RSQRT_SLOT.index(t) + 2)
                    link(v.tensor_scalar(hs[:, 0, :], hs[:, 1, :], 1.0 / HD, RMS_EPS, ALU.mult, ALU.add))
                    rsqrt_start(*heads_rsqrt())
                if t == SCALE_QK_SLOT:
                    dve.wait_ge(rsqrt_ready, 2)
                    for z in range(2):
                        v.tensor_tensor(heads_of(z), heads_of(z), head_scales(z), ALU.mult).then_inc(qk_scaled, 1)
                if t in M0_SLOTS:
                    for n in m0_units(t):
                        reduce_unit(0, n, first=True)
                        if n == MUN_A - 1:
                            split_maxima(0, 0, first=True)
            split_maxima(0, 1, first=True)

            run(0, first=True)
            with dve.Fori(0, 2) as i:
                for k in (1, 2, 3):
                    run(3 * i + k)
            run(7, last=True)
            take_sums(7, 1)
            gate_logits(0)
            normalise(7, 1, last=True)
            gate_weights(0)
            dve.wait_ge(turned, 2 * NG)

            for c in range(4):
                for i, (name, wn, nr, hb, src) in enumerate(MOE):
                    n = c * NB + i
                    for kind, t in TAIL[1].get(n, ()):
                        if kind == "proj":
                            add_projection(t)
                        if kind == "gate":
                            gate_logits(1)
                            gate_weights(1)
                    if n == X2_BLOCK:
                        norm_x2(1)
                    if name == "z1":
                        t1 = hid[:, SLOT[("z1", hb)], :]
                        dve.wait_ge(hb_read, n + 1)
                        v.scalar_tensor_tensor(out=t1, in0=t1, scalar=1.0, in1=ps[:, n % EB, :],
                                               op0=ALU.add, op1=ALU.mult).then_inc(glu_ready, 1)
                    if name == "z2":
                        t1 = hid[:, SLOT[("z1", hb)], :]
                        dve.wait_ge(hb_read, n + 1)
                        dve.wait_ge(glu_ready, 4 * c + hb + 1)
                        v.scalar_tensor_tensor(out=t1, in0=hid[:, SLOT[("z2", hb)], :], scalar=0.5, in1=t1,
                                               op0=ALU.mult, op1=ALU.mult).then_inc(glu_ready, 1)
                for t in range(4 * c, 4 * c + 4):
                    dve.wait_ge(down_done, t + 1)
                    for e in range(E):
                        ins = v.scalar_tensor_tensor(out=xs[:, t, ZM:D], in0=ps[:, 6 + t % 2, e * ZW:(e + 1) * ZW], scalar=gl[:, 3, t, e:e + 1],
                                                     in1=xs[:, t, ZM:D], op0=ALU.mult, op1=ALU.add)
                        if e < E - 1:
                            link(ins)
                        else:
                            ins.then_inc(out_ready, 1)

        @block.tensor
        def _(pe):
            mm = nc.tensor.matmul

            def turn(dst, src):
                return nc.tensor.transpose(dst, src, ident[:])

            pe.wait_ge(const_ready, 12)
            def turn_tiles(bank, c, first):
                for i in range(4):
                    pe.wait_ge(xn_ready, first + 4 * c + i + 1)
                    last = turn(ps[:, bank, i * P:(i + 1) * P], tmp[:, 4 * c + i, :])
                return last

            def values_of(bank, c):
                for i in range(4):
                    t = 4 * c + i
                    last = mm(ps[:, bank, i * P:(i + 1) * P], tT[:, t * P:(t + 1) * P], W("Wv"), start=True, stop=True)
                return last

            for c in range(2):
                turn_tiles(c, c, 0).then_inc(tr_done, 1)
            pe.wait_ge(wa_in, 16)
            for c in range(2):
                pe.wait_ge(tT_ready, c + 1)
                r = tT[:, c * CH:(c + 1) * CH]
                mm(ps[:, 2 + c, :], W("Wq"), r, start=True, stop=True).then_inc(q_done, 1)
                mm(ps[:, 4 + c, :], W("Wk"), r, start=True, stop=True).then_inc(k_done, 1)
                values_of(6 + c, c).then_inc(v_done, 1)

            def lane(item):
                kind, n = item
                b = lane_bank(item)
                bank = ps[:, b, :]
                before = LANE_BEFORE[item]
                if before:
                    read = {"xT": tT_ready, "q": q_ready, "k": k_ready, "v": v_ready, "hT": hT_ready, "qkv": qkv_read, "sp": spT_ready}
                    pe.wait_ge(read[before[0]], before[1] + 1)
                if kind == "xT":
                    turn_tiles(b, n, 0).then_inc(tr_done, 1)
                elif kind == "q":
                    pe.wait_ge(tT_ready, n + 1)
                    mm(bank, W("Wq"), tT[:, n * CH:(n + 1) * CH], start=True, stop=True).then_inc(q_done, 1)
                elif kind == "k":
                    mm(bank, W("Wk"), tT[:, n * CH:(n + 1) * CH], start=True, stop=True).then_inc(k_done, 1)
                elif kind == "v":
                    values_of(b, n).then_inc(v_done, 1)
                elif kind == "hT":
                    turn_tiles(b, n, NT).then_inc(hT_done, 1)
                elif kind == "qkv":
                    if n == 0:
                        pe.wait_ge(wf_in, 32)
                    pe.wait_ge(hT_ready, n // 4 + 1)
                    mm(bank[:, 0:3 * D], tT[:, n * P:(n + 1) * P], W("qkv"), start=True, stop=True).then_inc(qkv_done, 1)
                elif kind == "sp":
                    z, p = n // 3, n % 3
                    pe.wait_ge((hi_ready, mid_ready, lo_ready)[p], z + 1)
                    bb = bank.bitcast(BF16)
                    for s in range(2):
                        for i in range(4):
                            last = nc.tensor.transpose(bb[:, s * CH + i * P:s * CH + (i + 1) * P],
                                                       parts[:, z % 2, p, i, s * D:(s + 1) * D], identb[:])
                    last.then_inc(spT_done, 1)

            def max_unit(g, u, n, first=False):
                qi, j, nh, k0, wdt, diag = MUNITS[n]
                if first:
                    if n >= 3:
                        pe.wait_ge(m_reduced, n - 2)
                    bank = ps[:, FIRST_BANKS[n % 3], :]
                else:
                    bank = ps[:, turn_bank("m", n), :]
                for a in range(nh):
                    last = mm(bank[:, a * wdt:(a + 1) * wdt], qst[u][0:PADR, qi // 4, j + a, (qi % 4) * P:(qi % 4 + 1) * P],
                              kst[u][0:PADR, j + a, k0:k0 + wdt], start=True, stop=not diag)
                    if diag:
                        last = mm(bank[:, (a + 1) * wdt - P:(a + 1) * wdt], identb[:], maskb[:], start=False, stop=True)
                last.then_inc(m_scored, 1)

            def bank_free(g, what, n, first, last):
                if last:
                    if (what, n) == ("row", 1):
                        pe.wait_ge(m_reduced, NG * MUN)
                        pe.wait_ge(turned, 2 * g - 1)
                        pe.wait_ge(m_rows_ready, 2 * g + 1)
                    elif (what, n) == ("back", 1):
                        pe.wait_ge(m_rows_ready, 2 * g + 2)
                    else:
                        pe.wait_ge(turned, 2 * g)
                    return
                at = TURNS.index((what, n)) - len(TURN_BANKS)
                if first and at >= 0 and TURNS[at] == ("back", 1):
                    at -= len(TURN_BANKS)
                if first and at < 0:
                    pe.wait_ge(m_reduced, MUN)
                    pe.wait_ge(m_rows_ready, 1)
                    return
                r = g if at >= 0 else g - 1
                before, k = TURNS[at]
                if before == "m":
                    pe.wait_ge(m_reduced, (r + 1) * MUN + k + 1)
                elif before == "row":
                    pe.wait_ge(m_rows_ready, 2 * r + (2 if k == 1 else 3))
                else:
                    pe.wait_ge(turned, 2 * r + (0 if k == 1 else 1))

            def row_copy(g, h, bank=7):
                pe.wait_ge(m_parts, 2 * g + h + 1)
                bank = ps[:, bank, 0:64].bitcast(BF16)
                nc.tensor.transpose(bank, mxp[:, h].rearrange("p a b -> p (a b)"), identb[:]).then_inc(m_rows_done, 1)

            def back(g, c, bank):
                pe.wait_ge(avs_ready, 2 * g + c + 1)
                for i in range(4):
                    last = turn(ps[:, bank, i * P:(i + 1) * P], avs[:, c, i * P:(i + 1) * P])
                last.then_inc(back_done, 1)

            def values(g, u, s, first=False):
                c, kb, off, diag = KSTEPS[s]
                if kb == 0:
                    if not (first and c == 0):
                        pe.wait_ge(avs_ready, 2 * g + c)
                    if c == 0:
                        pe.wait_ge(vg_ready, g + 1)
                if diag:
                    nd = sum(KSTEPS[i][3] for i in range(s + 1))
                    pe.wait_ge(diag_done, g * DIAGS + 2 * nd)
                else:
                    pe.wait_ge(e_exped, g * EUNITS + 2 * s + 2)
                for j in range(HG):
                    last = mm(ps[32 * j:32 * j + 32, 6, off:CH], vg[u][:, kb, j, :], pt[:, s % 3, j, off:CH],
                              start=(kb == 0), stop=(kb == 4 * c + 3))
                last.then_inc(av_done, 1)

            def tail(item):
                kind, n = item
                bank = ps[:, tail_bank(item), :]
                before = TAIL_BEFORE[item]
                if before:
                    read = {"aoT": aoT_ready, "proj": x2_ready, "xfT": xfT_ready, "gate": gmax_ready}
                    pe.wait_ge(read[before[0]], before[1] + 1)
                elif kind == "aoT":
                    pe.wait_ge(m_reduced, NG * MUN)
                    pe.wait_ge(m_rows_ready, 2 * NG - 1)
                    pe.wait_ge(turned, 2 * NG - 3)
                if kind == "aoT":
                    if n % 2 == 0:
                        pe.wait_ge(turned, NG * (n // 2 + 1))
                    for i in range(4):
                        b, qi = n // 2, (4 * n + i) % TB
                        last = turn(bank[:, i * P:(i + 1) * P], ao[:, qi, b * D:(b + 1) * D])
                    last.then_inc(aoT_done, 1)
                elif kind == "proj":
                    pe.wait_ge(aoT_ready, n // 4 + 1)
                    mm(bank[:, 0:ZW], tT[:, n * P:(n + 1) * P], W("wo", ZM, D), start=True, stop=True).then_inc(proj_done, 1)
                elif kind == "xfT":
                    for i in range(4):
                        pe.wait_ge(xf_ready, 4 * n + i + 1)
                        last = turn(bank[:, i * P:(i + 1) * P], tmp[:, 4 * n + i, :])
                    last.then_inc(xfT_done, 1)
                elif kind == "gate":
                    pe.wait_ge(xfT_ready, 2 * n + 2)
                    for i in range(TB):
                        t = n * TB + i
                        last = mm(bank[:, i * E:(i + 1) * E], tT[:, t * P:(t + 1) * P], W("gate"), start=True, stop=True)
                    last.then_inc(gate_done, 1)

            def run(g, stacks_of_next, u, first=False, last=False):
                for s, (c, kb, off, diag) in enumerate(KSTEPS):
                    if s == 0:
                        pe.wait_ge(rows_in[0], 16 * (g + 1))
                    if s == 4:
                        pe.wait_ge(rows_in[1], 16 * (g + 1))
                    if s == 0 and not last:
                        pe.wait_ge(stack_in[(u + 1) % NBUF], stacks_of_next)
                    for what, n in order_of_step(s, not last):
                        if what == "m":
                            bank_free(g, "m", n, first, last)
                            max_unit(g + 1, (u + 1) % NBUF, n)
                        elif what == "e":
                            if not (first and s == 0):
                                pe.wait_ge(e_exped, g * EUNITS + 2 * s + n - 1)
                            for j in (2 * n, 2 * n + 1):
                                ins = mm(ps[:, j, off:CH], kst[u][0:EROWS, j, kb * P:(kb + 1) * P], qst[u][0:EROWS, c, j, off:CH],
                                         start=True, stop=True)
                            ins.then_inc(e_scored, 1)
                        elif s >= LAG:
                            values(g, u, s - LAG, first)
                        elif not first:
                            values(g - 1, (u - 1) % NBUF, STEPS + s - LAG)
                    if s == 1:
                        bank_free(g, "row", 1, first, last)
                        row_copy(g, 1, turn_bank("row", 1, last))
                    if s == BACK1_STEP and not first:
                        bank_free(g, "back", 1, first, last)
                        back(g - 1, 1, turn_bank("back", 1, last))
                    if s == MROWS_STEP and not last:
                        bank_free(g, "row", 0, first, last)
                        row_copy(g + 1, 0, turn_bank("row", 0))
                    if s == BACK0_STEP:
                        bank_free(g, "back", 0, first, last)
                        back(g, 0, turn_bank("back", 0, last))
                    if last:
                        for item in TAIL[0].get(s, ()):
                            tail(item)
            def first_max_unit(n):
                if n == 0:
                    pe.wait_ge(stack_in[0], STACK_DMAS)
                    pe.wait_ge(x1_ready, NT)
                max_unit(0, 0, n, first=True)
                if n == MUN_A + 4:
                    row_copy(0, 0)

            for t in range(FRONT):
                lanes = LANE[t] + [None] * 3
                if 4 <= t < NT + 4:
                    n = t - 4
                    pe.wait_ge(aT_ready, n + 1)
                    mm(ps[:, 6, 0:D], aT[:, n % 2, :], W("Wo"), start=True, stop=True).then_inc(wo_done, 1)
                if t < NT:
                    b, qi = t // TB, t % TB
                    if t in (0, TB):
                        for ready in (q_ready, k_ready, v_ready):
                            pe.wait_ge(ready, 2 * b + 2)
                    if t >= 2:
                        pe.wait_ge(exped, t - 1)
                    for k0 in range(0, P * (qi + 1), CH):
                        n = min(CH, P * (qi + 1) - k0)
                        bank = ps[:, 2 * (t % 2) + k0 // CH, :]
                        diag = k0 + n == P * (qi + 1)
                        last = mm(bank[:, 0:n], qT[:, t * P:(t + 1) * P], kT[:, b * T + k0:b * T + k0 + n], start=True, stop=not diag)
                        if diag:
                            last = mm(bank[:, n - P:n], identb[:], maskb[:], start=False, stop=True)
                    last.then_inc(scored, 1)
                if lanes[0]:
                    lane(lanes[0])
                if 3 <= t < NT + 3:
                    n = t - 3
                    pe.wait_ge(pT_ready, n + 1)
                    if n >= 1:
                        pe.wait_ge(x1_ready, n)
                    nk = n % TB + 1
                    for kb in range(nk):
                        last = mm(ps[:, 6, 0:P], vv[:, (n // TB) * TB + kb, :], pselT[:, n % 2, kb * P:(kb + 1) * P],
                                  start=(kb == 0), stop=(kb == nk - 1))
                    last.then_inc(av_a, 1)
                if lanes[1]:
                    lane(lanes[1])
                if 2 <= t < NT + 2:
                    n = t - 2
                    pe.wait_ge(psel_ready, n + 1)
                    if n >= 1:
                        pe.wait_ge(pT_ready, n)
                    for kb in range(n % TB + 1):
                        last = turn(ps[:, 4 + kb // 4, (kb % 4) * P:(kb % 4 + 1) * P], psel[:, n % 2, kb * P:(kb + 1) * P])
                    last.then_inc(pT_done, 1)
                units = list(m0_units(t)) if t in M0_SLOTS else []
                for item in lanes[2:]:
                    if item:
                        lane(item)
                    if units and t > M0_SLOTS[0]:
                        first_max_unit(units.pop(0))
                for n in units:
                    first_max_unit(n)
            pe.wait_ge(spT_ready, 12)
            run(0, STACK_DMAS, 0, first=True)
            with pe.Fori(0, 2) as i:
                run(3 * i + 1, STACK_DMAS * (i + 1), 1)
                run(3 * i + 2, STACK_DMAS * (i + 2), 2)
                run(3 * i + 3, STACK_DMAS * (i + 2), 0)
            run(7, None, 1, last=True)
            for s in range(STEPS - LAG, STEPS):
                values(7, 1, s)

            for c in range(4):
                r = tT[:, c * CH:(c + 1) * CH]
                for i, (name, wn, nr, hb, src) in enumerate(MOE):
                    n = c * NB + i
                    for item in TAIL[1].get(n, ()):
                        tail(item)
                    if n == BACK_BLOCK:
                        pe.wait_ge(turned, 2 * NG - 1)
                        back(NG - 1, 1, 7)
                    if n == 0:
                        pe.wait_ge(xfT_ready, 2)
                        pe.wait_ge(e_exped, NG * EUNITS)
                    if n >= EB:
                        m = n - EB
                        pe.wait_ge(hb_read, m + 1)
                        if MOE[m % NB][0] == "z1":
                            pe.wait_ge(glu_ready, 4 * (m // NB) + MOE[m % NB][3] + 1)
                    if i == 0:
                        pe.wait_ge(xfT_ready, c + 1)
                    if src:
                        pe.wait_ge(hb_read, c * NB + ORDER[(src, nr - 1)] + 1)
                    for q in range(nr):
                        if nr == 1:
                            wt, rr = W(wn, hb * P, (hb + 1) * P), (hid[:, SLOT[(src, 0)], :] if src else r)
                        else:
                            wt, rr = V(wn, q, hb * P, (hb + 1) * P), hid[:, SLOT[(src, q)], :]
                        ins = mm(ps[:, n % EB, :], wt, rr, start=(q == 0), stop=(q == nr - 1))
                    ins.then_inc(hb_done, 1)
                for t in range(4 * c, 4 * c + 4):
                    if t < 2:
                        pe.wait_ge(turned, 2 * NG)
                    else:
                        pe.wait_ge(out_ready, t - 1)
                    cc = (t % 4) * P
                    for e, hn, wn in ((0, "h0", "e0_down"), (1, "z1", "e1_down"), (3, "u3", "e3_out"), (2, "a3", "e2_l4")):
                        if t == 4 * c and hn == "z1":
                            pe.wait_ge(glu_ready, 4 * (c + 1))
                        elif t == 4 * c:
                            pe.wait_ge(hb_read, NB * c + ORDER[(hn, 1)] + 1)
                        for q in range(2):
                            ins = mm(ps[:, 6 + t % 2, e * ZW:(e + 1) * ZW], hid[:, SLOT[(hn, q)], cc:cc + P], V(wn, q, ZM, D),
                                     start=(q == 0), stop=(q == 1))
                    ins.then_inc(down_done, 1)


_A = ("Wq", "Wk", "Wv", "Wo")


def kernel(**inputs):
    import numpy as np
    import concourse.bacc as bacc
    from concourse.bass_utils import run_bass_kernel_spmd

    def a(n):
        return np.asarray(inputs["L0_attn_" + n])

    def f(n):
        return np.asarray(inputs["L0_ffn_" + n])

    arrays = {
        "x": np.ascontiguousarray(a("summaries")),
        "wts": np.ascontiguousarray(np.concatenate(
            [a(n) for n in _A] + [f(n).T for n in ("wq", "wk", "wv", "wo", "gate_w", "e0_up", "e1_w1", "e1_w2", "e2_l1", "e3_down", "e3_up")], axis=1)),
        "wts2": np.ascontiguousarray(np.concatenate(
            [f(n).T for n in ("e0_down", "e1_down", "e2_l2", "e2_l3", "e2_l4", "e3_out")], axis=1)),
        "cols": np.ascontiguousarray(np.stack([a("bq"), a("bk"), f("n1_w"), f("n2_w")], axis=1)),
        "rows": np.ascontiguousarray(np.concatenate([a("bv"), a("bo"), f("qn_w"), f("kn_w")])[None]),
    }
    nc = bacc.Bacc("TRN2", target_bir_lowering=False, num_devices=1)
    args = [nc.dram_tensor("in_" + n, v.shape, mybir.dt.from_np(v.dtype), kind="ExternalInput").ap() for n, v in arrays.items()]
    args.append(nc.dram_tensor("out", (B, T, D), F32, kind="ExternalOutput").ap())
    build(nc, *args)
    r = run_bass_kernel_spmd(nc, [{"in_" + n: v for n, v in arrays.items()}], core_ids=[0])
    return r.results[0]["out"]
```
